# Optimizing a Trainium2 kernel written in Bass

```python
import numpy as np
import jax
import jax.numpy as jnp

def _softmax(x, axis=-1):
    return jax.nn.softmax(x, axis=axis)

def _gelu(x):
    return jax.nn.gelu(x, approximate=True)

def _silu(x):
    return jax.nn.silu(x)

def _sigmoid(x):
    return jax.nn.sigmoid(x)

def _layernorm(x, axis=-1, eps=1e-05):
    m = jnp.mean(x, axis=axis, keepdims=True)
    v = jnp.var(x, axis=axis, keepdims=True)
    return (x - m) / jnp.sqrt(v + eps)

def _scatter_add(tgt, idx, src, axis=0):
    return tgt.at[idx].add(src)

def _segment_sum(src, seg, n):
    return jax.ops.segment_sum(src, seg, n)
kernel_name = 'mk_xattn_ffn_d1_seqx_r2_356b4e'

def setup_inputs(seed: int=0):
    np.random.seed(seed)
    _w = jnp.asarray

    def _rec_inputs():
        import jax
        import jax.numpy as jnp
        _rk = jax.random.key(seed)
        x = -0.0003929 + 0.9999 * jax.random.normal(jax.random.fold_in(_rk, 1), (16, 256, 2048), jnp.float32)
        _lenS = 256 - jax.random.randint(jax.random.fold_in(_rk, 7), (16,), 0, max(1, 256 // 4) + 1, jnp.int32)
        _lenS2 = 256 - jax.random.randint(jax.random.fold_in(_rk, 8), (16,), 0, max(1, 256 // 4) + 1, jnp.int32)
        _ctx_1024P = jax.random.normal(jax.random.fold_in(_rk, 11), (16, 16, 512), jnp.float32)
        _ctx_1024c = jax.random.dirichlet(jax.random.fold_in(_rk, 511), 0.3 * jnp.ones((16,), jnp.float32), (16, 256))
        _ctx_1024t = jnp.einsum('bsk,bkd->bsd', _ctx_1024c, _ctx_1024P)
        _ctx_1024t = _ctx_1024t * jax.lax.rsqrt(jnp.mean(jnp.square(_ctx_1024t)) + 1e-12) * 0.953939
        ctx_1024 = -1.39393e-06 + 0.999914 * (_ctx_1024t + 0.3 * jax.random.normal(jax.random.fold_in(_rk, 611), (16, 256, 512), jnp.float32))
        return (x, ctx_1024)
    x, ctx_1024 = _rec_inputs()

    def _L0_xattn_setup():
        import jax, jax.numpy as jnp
        import numpy as np
        import math
        DIM_V = 256
        key = jax.random.key(seed)
        k1, k2, k3, k4, k5, k6 = jax.random.split(key, 6)
        B, C, N, M = (8, DIM_V, 2048, 512)
        pcd_up = jax.random.normal(k1, (B, C, N), dtype=jnp.float32)
        pcd_down = jax.random.normal(k2, (B, C, M), dtype=jnp.float32)
        s = 1.0 / math.sqrt(C)
        Wq = jax.random.normal(k3, (C, C), dtype=jnp.float32) * s
        Wk = jax.random.normal(k4, (C, C), dtype=jnp.float32) * s
        Wv = jax.random.normal(k5, (C, C), dtype=jnp.float32) * s
        Wskip = jax.random.normal(k6, (C, C), dtype=jnp.float32) * s
        return {'pcd_up': pcd_up, 'pcd_down': pcd_down, 'Wq': Wq, 'Wk': Wk, 'Wv': Wv, 'Wskip': Wskip}
    _L0_xattn_all = _L0_xattn_setup()
    _L0_xattn_in = {k: v for k, v in _L0_xattn_all.items() if k in ('Wq', 'Wk', 'Wv', 'Wskip')}
    del _L0_xattn_all

    def _L0_ffn_setup():
        import jax, jax.numpy as jnp
        import numpy as np
        B_, S, D_IN, D_OUT = (4, 1024, 2048, 2048)
        N, RANK, ALPHA = (8, 16, 32)
        SCALE = ALPHA / RANK
        key = jax.random.key(seed)
        kx, ka, kb, kw, kbias = jax.random.split(key, 5)
        x = jax.random.normal(kx, (B_, S, D_IN), dtype=jnp.float32)
        lora_A = jax.random.normal(ka, (N, RANK, D_IN), dtype=jnp.float32) * (1.0 / np.sqrt(D_IN))
        lora_B = jax.random.normal(kb, (N, D_OUT, RANK), dtype=jnp.float32) * (1.0 / np.sqrt(RANK))
        W = jax.random.normal(kw, (D_OUT, D_IN), dtype=jnp.float32) * (1.0 / np.sqrt(D_IN))
        bias = jax.random.normal(kbias, (D_OUT,), dtype=jnp.float32) * 0.01
        lora_weights = jnp.full((N,), 1.0 / N, dtype=jnp.float32)
        return {'x': x, 'lora_A': lora_A, 'lora_B': lora_B, 'W': W, 'bias': bias, 'lora_weights': lora_weights}
    _L0_ffn_all = _L0_ffn_setup()
    _L0_ffn_in = {k: v for k, v in _L0_ffn_all.items() if k in ('lora_A', 'lora_B', 'W', 'bias', 'lora_weights')}
    del _L0_ffn_all
    return {'x': x, 'ctx_1024': ctx_1024, 'L0_xattn_Wq': _L0_xattn_in['Wq'], 'L0_xattn_Wk': _L0_xattn_in['Wk'], 'L0_xattn_Wv': _L0_xattn_in['Wv'], 'L0_xattn_Wskip': _L0_xattn_in['Wskip'], 'L0_ffn_lora_A': _L0_ffn_in['lora_A'], 'L0_ffn_lora_B': _L0_ffn_in['lora_B'], 'L0_ffn_W': _L0_ffn_in['W'], 'L0_ffn_bias': _L0_ffn_in['bias'], 'L0_ffn_lora_weights': _L0_ffn_in['lora_weights']}

def reference(x, ctx_1024, L0_xattn_Wq, L0_xattn_Wk, L0_xattn_Wv, L0_xattn_Wskip, L0_ffn_lora_A, L0_ffn_lora_B, L0_ffn_W, L0_ffn_bias, L0_ffn_lora_weights):
    import jax
    import jax.numpy as jnp

    def _L0_xattn_ref(pcd_up, pcd_down, Wq, Wk, Wv, Wskip):
        import jax, jax.numpy as jnp
        import numpy as np
        import math
        DIM_V = 256
        q = jnp.einsum('oc,bcn->bon', Wq, pcd_up)
        k = jnp.einsum('oc,bcm->bom', Wk, pcd_down)
        v = jnp.einsum('oc,bcm->bom', Wv, pcd_down)
        C = q.shape[1]
        scale = jnp.sqrt(jnp.asarray(C, dtype=q.dtype))
        energy = jnp.einsum('bcn,bcm->bnm', q, k) / scale
        attention = jax.nn.softmax(energy, axis=-1)
        x = jnp.einsum('bnm,bcm->bcn', attention, v)
        skip = jnp.einsum('oc,bcn->bon', Wskip, pcd_up)
        return skip + x

    def _L0_ffn_ref(x, lora_A, lora_B, W, bias, lora_weights):
        import jax, jax.numpy as jnp
        import numpy as np
        B_, S, D_IN, D_OUT = (4, 1024, 2048, 2048)
        N, RANK, ALPHA = (8, 16, 32)
        SCALE = ALPHA / RANK
        h = jnp.einsum('bsd,nrd->nbsr', x, lora_A)
        coef = (SCALE * lora_weights)[:, None, None]
        lora_out = jnp.einsum('nbsr,nor->bso', h, lora_B * coef)
        base = jnp.einsum('bsd,od->bso', x, W) + bias
        return base + lora_out
    x = x + _L0_xattn_ref(_layernorm(x, axis=-1), ctx_1024, L0_xattn_Wq, L0_xattn_Wk, L0_xattn_Wv, L0_xattn_Wskip)
    x = x + _L0_ffn_ref(_layernorm(x, axis=-1), L0_ffn_lora_A, L0_ffn_lora_B, L0_ffn_W, L0_ffn_bias, L0_ffn_lora_weights)
    return x

_drawn_inputs = setup_inputs


def setup_inputs(seed=0):
    import zlib

    import numpy as np

    out = dict(_drawn_inputs(seed))
    spreads = {'L0_ffn_lora_weights': (0.125, 0.2)}
    factors = {'L0_ffn_bias': 8.0}
    for name, (base, spread) in spreads.items():
        noise = np.random.default_rng([zlib.crc32(name.encode()), seed]).standard_normal(out[name].shape)
        drawn = base * np.exp(spread * noise) if base else spread * noise
        out[name] = jnp.asarray(drawn.astype(out[name].dtype))
    for name, factor in factors.items():
        out[name] = (out[name] * factor).astype(out[name].dtype)
    return out
```

```python
from collections import namedtuple
from contextlib import ExitStack

import concourse.bass as bass
from concourse import mybir


P = 128
NC = 512
EPS = 1e-5
LORA_SCALE = 2.0
XS = 2.0 ** 10
PS = 2.0 ** 14
TOP = 2.0 ** 14
TINY = 2.0 ** -100

ALU = mybir.AluOpType
ACT = mybir.ActivationFunctionType
AX_X = mybir.AxisListType.X
F16 = mybir.dt.float16
F32 = mybir.dt.float32
U32 = mybir.dt.uint32
ABSMAX = bass.bass_isa.ReduceOp.absmax
EXPONENT = 0x7F800000

Step = namedtuple("Step", "g b h p j")


def xattn_ffn(nc, x, ctx_, wq, wk, wvT, wskipT, lora_a, lora_bT, lora_w, wT, bias, x1, out):
    B, C, N = x.shape
    M = ctx_.shape[2]
    R = lora_a.shape[0]
    CT, MT, KT, OC = C // P, M // P, N // P, N // NC
    STEPS = N // NC
    NT = NC // P
    ROWS = B * C // P
    assert CT == 2 and M == NC and R == P and STEPS == 4 and B % 2 == 0 and ROWS % 2 == 0

    def step(b, h, p, j):
        return Step(STEPS * b + j, b, h, p, j)

    def after(s, n=1):
        for _ in range(n):
            if s.j < STEPS - 1:
                s = Step(s.g + 1, s.b, s.h, s.p, s.j + 1)
            else:
                s = Step(s.g + 1, s.b + 1, s.h + s.p, 1 - s.p, 0)
        return s

    def batches(eng, body):
        with eng.Fori(0, B // 2 - 1) as i:
            for p in range(2):
                for j in range(STEPS):
                    body(step(2 * i + p, i, p, j), 2)
        for p in range(2):
            for j in range(STEPS):
                body(step(B - 2 + p, B // 2 - 1, p, j), 1 - p)

    with ExitStack() as stack:
        def sb(name, shape, dt, where=None):
            return (where or stack).enter_context(nc.sbuf_tensor(name, shape, dt))

        def sem(name):
            return stack.enter_context(nc.semaphore(name))

        bank = [stack.enter_context(nc.psum_tensor(f"bank{i}", [P, NC], F32)) for i in range(8)]

        W = sb("W", [P, KT, 2, N], F16)

        def spare(k0, k1):
            return W[:, k0:k1].rearrange("p k s n -> p (k s n)").bitcast(F32)

        xbuf = [spare(KT - 4 + 2 * p, KT - 2 + 2 * p).rearrange("p (t n) -> p t n", t=CT) for p in range(2)]
        raw = spare(KT - 5, KT - 4).rearrange("p (v n) -> p v n", v=2)

        ident = sb("ident", [P, P], F32)
        lora_b_sb = sb("lora_b_sb", [P, N], F32)
        coef = sb("coef", [P, 1], F32)
        carrier = sb("carrier", [P, 1], F32)
        wmax = sb("wmax", [P, KT], F32)

        with ExitStack() as a:
            qk_w = sb("qk_w", [P, 2, CT, C], F32, a)
            mT = sb("mT", [P, CT, C], F32, a)
            wv_sb = sb("wv_sb", [P, CT, C], F32, a)
            wsk_raw = sb("wsk_raw", [P, CT, C], F32, a)
            wsk = sb("wsk", [P, 2, CT, C], F16, a)
            ctx_sb = sb("ctx_sb", [P, CT, M], F32, a)
            xn32 = sb("xn32", [P, CT, NC], F32, a)
            xn = sb("xn", [P, 2, 2, CT, NC], F16, a)
            kk = sb("kk", [P, 2, 2, CT, M], F16, a)
            vT = sb("vT", [P, 2, 2, MT, C], F16, a)
            prob = sb("prob", [P, NT, M], F32, a)
            pT = sb("pT", [P, 2, MT, NC], F16, a)
            skip32 = sb("skip32", [P, CT, NC], F32, a)
            stats = sb("stats", [P, CT, STEPS, 6], F32, a)
            mv = sb("mv", [P, 2, CT, 2], F32, a)
            veps = sb("veps", [P, CT], F32, a)
            half = sb("half", [P, CT], F32, a)
            rstd = sb("rstd", [P, 2, CT], F32, a)
            amax = sb("amax", [P, 2], F32, a)
            gmax = sb("gmax", [P, 2], F32, a)
            cmax = sb("cmax", [P, 2], F32, a)
            pow2 = sb("pow2", [P, 2], F32, a)
            unscale = sb("unscale", [P, 2], F32, a)
            kvscale = sb("kvscale", [P, 2], F32, a)
            escale = sb("escale", [P, 2], F32, a)
            vscale = sb("vscale", [P, 2], F32, a)
            wsk_sc = sb("wsk_sc", [P, 8], F32, a)
            rowmax = sb("rowmax", [P, NT], F32, a)
            nmax = sb("nmax", [P, NT], F32, a)
            rsum = sb("rsum", [P, NT], F32, a)
            rinv = sb("rinv", [P, NT], F32, a)
            KV_STEPS = 6
            ebank, sbank, abank = bank[0:4], bank[4:6], bank[6:8]

            w_in = sem("w_in")
            wv_in = sem("wv_in")
            lora_in = sem("lora_in")
            x_in = [[sem(f"x_in{p}{j}") for j in range(STEPS)] for p in range(2)]
            ctx_in = sem("ctx_in")
            x1_out = sem("x1_out")
            ident_zero, ident_ok = sem("ident_zero"), sem("ident_ok")
            half_ok, lora_b_ok = sem("half_ok"), sem("lora_b_ok")
            mT_done, mT_ok = sem("mT_done"), sem("mT_ok")
            wsk_max, wsk_all, wsk_step = sem("wsk_max"), sem("wsk_all"), sem("wsk_step")
            wsk_hi, wsk_lo = sem("wsk_hi"), sem("wsk_lo")
            bn_done, mv_done, veps_done = sem("bn_done"), sem("mv_done"), sem("veps_done")
            rstd_done = sem("rstd_done")
            kk_done, v_done = sem("kk_done"), sem("v_done")
            kk_raw, v_raw = sem("kk_raw"), sem("v_raw")
            kv_max, kv_all, kv_step = sem("kv_max"), sem("kv_all"), sem("kv_step")
            kv_hi, kv_lo = sem("kv_hi"), sem("kv_lo")
            xn_done, xn_hi, xn_lo = sem("xn_done"), sem("xn_hi"), sem("xn_lo")
            skip_done, skip_out, x1a = sem("skip_done"), sem("skip_out"), sem("x1a")
            att_done, x1b = sem("att_done"), sem("x1b")
            e_done, max_done, nmax_done = sem("e_done"), sem("max_done"), sem("nmax_done")
            exp_done, rinv_done, prob_done = sem("exp_done"), sem("rinv_done"), sem("prob_done")
            t_done, pT_hi, pT_lo = sem("t_done"), sem("pT_hi"), sem("pT_lo")

            x_v = x.rearrange("b (t p) n -> b p t n", p=P)
            x1_v = x1.rearrange("b (t p) n -> b p t n", p=P)
            ctx_v = ctx_.rearrange("b (t p) m -> b p t m", p=P)

            block = a.enter_context(nc.Block())

            @block.sync
            def _(sp):
                for b in range(2):
                    for j in range(STEPS):
                        cols = slice(j * NC, (j + 1) * NC)
                        sp.dma_start(xbuf[b][:, :, cols], x_v[b][:, :, cols]).then_inc(x_in[b][j], 16)
                sp.wait_ge(v_done, 1)
                sp.dma_start(ctx_sb[:], ctx_v[1]).then_inc(ctx_in, 16)

                def body(s, ahead):
                    cols = slice(s.j * NC, (s.j + 1) * NC)
                    sp.wait_ge(x1b, CT * (s.g + 1))
                    sp.dma_start(x1_v[s.b][:, :, cols], xbuf[s.p][:, :, cols]).then_inc(x1_out, 16)
                    sp.wait_ge(x1_out, 16 * (s.g + 1))
                    if ahead == 2:
                        sp.dma_start(xbuf[s.p][:, :, cols], x_v[s.b + 2][:, :, cols]).then_inc(x_in[s.p][s.j], 16)
                        if s.j == 0:
                            sp.wait_ge(v_done, s.b + 2)
                            sp.dma_start(ctx_sb[:], ctx_v[s.b + 2]).then_inc(ctx_in, 16)

                batches(sp, body)

            @block.scalar
            def _(act):
                act.dma_start(ctx_sb[:], ctx_v[0]).then_inc(ctx_in, 16)
                act.dma_start(qk_w[:, 0], wq.rearrange("(t p) c -> p t c", p=P)).then_inc(w_in, 16)
                act.dma_start(qk_w[:, 1], wk.rearrange("(t p) c -> p t c", p=P)).then_inc(w_in, 16)
                act.dma_start(wv_sb[:], wvT.rearrange("(t p) c -> p t c", p=P)).then_inc(wv_in, 16)
                act.dma_start(wsk_raw[:], wskipT.rearrange("(t p) c -> p t c", p=P)).then_inc(wv_in, 16)
                act.dma_start(lora_b_sb[:], lora_bT).then_inc(lora_in, 16)
                act.dma_start(coef[:], lora_w).then_inc(lora_in, 16)
                act.wait_ge(mT_done, CT)
                for t in range(CT):
                    last = act.activation(mT[:, t, :], sbank[t][:, 0:C], ACT.Copy)
                last.then_inc(mT_ok, 1)

                def keys_values_raw(b):
                    act.wait_ge(kk_done, b + 1)
                    for t in range(CT):
                        last = act.activation(raw[:, 0, t * M:(t + 1) * M], sbank[t][:, :], ACT.Copy)
                    last.then_inc(kk_raw, 1)
                    act.wait_ge(v_done, b + 1)
                    for t in range(2):
                        last = act.activation(raw[:, 1, t * NC:(t + 1) * NC], abank[t][:, :], ACT.Copy)
                    last.then_inc(v_raw, 1)

                def keys_values_hi(b, p):
                    act.wait_ge(kv_step, KV_STEPS * b + 4)
                    for v, dst in enumerate((kk, vT)):
                        act.activation(dst[:, p, 0].rearrange("p t n -> p (t n)"), raw[:, v, :], ACT.Copy,
                                       scale=kvscale[:, v:v + 1]).then_inc(kv_hi, 1)

                def exponentials(s):
                    for t in range(NT):
                        act.wait_ge(nmax_done, NT * s.g + t + 1)
                        act.activation(prob[:, t, :], ebank[t][:, :], ACT.Exp, bias=nmax[:, t:t + 1],
                                       scale=escale[:, s.p:s.p + 1], accum_out=rsum[:, t:t + 1]).then_inc(exp_done, 1)

                def xn_hi_of(s):
                    for t in range(CT):
                        act.wait_ge(xn_done, CT * s.g + t + 1)
                        act.activation(xn[:, s.j % 2, 0, t, :], xn32[:, t, :], ACT.Copy).then_inc(xn_hi, 1)

                first = step(0, 0, 0, 0)
                xn_hi_of(first)
                act.wait_ge(wsk_step, 4)
                act.activation(wsk[:, 0].rearrange("p t c -> p (t c)"), wsk_raw[:].rearrange("p t c -> p (t c)"),
                               ACT.Copy, scale=wsk_sc[:, 5:6]).then_inc(wsk_hi, 1)
                xn_hi_of(after(first))
                keys_values_raw(0)
                keys_values_hi(0, 0)
                exponentials(first)

                def body(s, ahead):
                    for t in range(NT):
                        act.wait_ge(t_done, NT * s.g + t + 1)
                        act.activation(pT[:, 0, :, t * P:(t + 1) * P],
                                       ebank[t][:, :].rearrange("p (m n) -> p m n", m=MT), ACT.Copy).then_inc(pT_hi, 1)
                    act.wait_ge(pT_lo, NT * s.g + 1)
                    for t in range(CT):
                        act.wait_ge(skip_done, CT * s.g + t + 1)
                        act.activation(skip32[:, t, :], sbank[t][:, :], ACT.Copy,
                                       scale=wsk_sc[:, 6:7]).then_inc(skip_out, 1)
                    last = ahead == 0
                    if not (last and s.j == 3):
                        exponentials(after(s))
                    if not (last and s.j >= 2):
                        xn_hi_of(after(s, 2))
                    if ahead and s.j == 0:
                        keys_values_raw(s.b + 1)
                    if ahead and s.j == 2:
                        keys_values_hi(s.b + 1, 1 - s.p)

                batches(act, body)

            @block.gpsimd
            def _(pool):
                pool.memset(ident[:], 0.0).then_inc(ident_zero, 1)
                pool.wait_ge(ident_zero, 1)
                pool.affine_select(out=ident[:], in_=ident[:], compare_op=ALU.not_equal, fill=1.0, base=0,
                                   pattern=[[-1, P]], channel_multiplier=1).then_inc(ident_ok, 1)
                pool.memset(half[:], -0.5).then_inc(half_ok, 1)
                pool.wait_ge(half_ok, 1)

                def inverse_deviation(b, p):
                    pool.wait_ge(veps_done, b + 1)
                    pool.tensor_tensor(rstd[:, p, :], veps[:], half[:], ALU.pow).then_inc(rstd_done, 1)

                def keys_values_max():
                    pool.partition_all_reduce(gmax[:], amax[:], P, ABSMAX).then_inc(kv_all, 1)

                def normalised_lo(s):
                    for t in range(CT):
                        pool.wait_ge(xn_hi, CT * s.g + t + 1)
                        pool.tensor_tensor(xn[:, s.j % 2, 1, t, :], xn32[:, t, :], xn[:, s.j % 2, 0, t, :],
                                           ALU.subtract).then_inc(xn_lo, 1)

                first = step(0, 0, 0, 0)
                inverse_deviation(0, 0)
                normalised_lo(first)
                pool.wait_ge(wsk_max, 1)
                pool.partition_all_reduce(wsk_sc[:, 1:2], wsk_sc[:, 0:1], P, ABSMAX).then_inc(wsk_all, 1)
                normalised_lo(after(first))
                pool.wait_ge(kv_max, 2)
                keys_values_max()

                def body(s, ahead):
                    last = ahead == 0
                    cols = slice(s.j * NC, (s.j + 1) * NC)
                    for t in range(CT):
                        pool.wait_ge(skip_out, CT * s.g + t + 1)
                        pool.tensor_tensor(xbuf[s.p][:, t, cols], xbuf[s.p][:, t, cols], skip32[:, t, :],
                                           ALU.add).then_inc(x1a, 1)
                    if not (last and s.j >= 2):
                        normalised_lo(after(s, 2))
                    if ahead and s.j == 1:
                        pool.wait_ge(kv_max, 2 * (s.b + 2))
                        inverse_deviation(s.b + 1, 1 - s.p)
                        keys_values_max()

                batches(pool, body)

            @block.vector
            def _(dve):
                def chunk_stats(b, h, p, j):
                    dve.wait_ge(x_in[p][j], 16 * (h + 1))
                    for t in range(CT):
                        dve.bn_stats(stats[:, t, j, :], xbuf[p][:, t, j * NC:(j + 1) * NC]).then_inc(bn_done, 1)

                def batch_stats(b, p):
                    dve.wait_ge(bn_done, CT * STEPS * (b + 1))
                    dve.memset(carrier[:], 0.0)
                    for t in range(CT):
                        dve.bn_aggr(mv[:, p, t, :], stats[:, t].rearrange("p j s -> p (j s)")).then_inc(mv_done, 1)
                    dve.wait_ge(mv_done, CT * (b + 1))
                    dve.tensor_scalar(veps[:], mv[:, p, :, 1], EPS, XS ** -2, ALU.add, ALU.mult).then_inc(veps_done, 1)

                def normalise(s):
                    dve.wait_ge(rstd_done, s.b + 1)
                    dve.wait_ge(xn_lo, CT * s.g)
                    for t in range(CT):
                        dve.tensor_scalar(xn32[:, t, :], xbuf[s.p][:, t, s.j * NC:(s.j + 1) * NC],
                                          mv[:, s.p, t, 0:1], rstd[:, s.p, t:t + 1],
                                          ALU.subtract, ALU.mult).then_inc(xn_done, 1)

                def keys_values_amax(b):
                    for v, ready in enumerate((kk_raw, v_raw)):
                        dve.wait_ge(ready, b + 1)
                        dve.tensor_reduce(amax[:, v:v + 1], raw[:, v, :], AX_X, ALU.max,
                                          apply_absolute_value=True).then_inc(kv_max, 1)

                def keys_values_scales(b, p):
                    k = KV_STEPS * b
                    dve.wait_ge(kv_all, b + 1)
                    dve.tensor_scalar(cmax[:], gmax[:], TINY, None, ALU.max).then_inc(kv_step, 1)
                    dve.wait_ge(kv_step, k + 1)
                    dve.tensor_scalar(pow2[:].bitcast(U32), cmax[:].bitcast(U32), EXPONENT, None,
                                      ALU.bitwise_and).then_inc(kv_step, 1)
                    dve.wait_ge(kv_step, k + 2)
                    dve.tensor_scalar(unscale[:], pow2[:], 1.0 / TOP, None, ALU.mult).then_inc(kv_step, 1)
                    dve.wait_ge(kv_step, k + 3)
                    dve.reciprocal(kvscale[:], unscale[:]).then_inc(kv_step, 1)
                    dve.tensor_scalar(escale[:, p:p + 1], unscale[:, 0:1], 1.0 / (XS * C ** 0.5), None,
                                      ALU.mult).then_inc(kv_step, 1)
                    dve.tensor_scalar(vscale[:, p:p + 1], unscale[:, 1:2], 1.0 / PS, None,
                                      ALU.mult).then_inc(kv_step, 1)
                    dve.wait_ge(kv_step, k + KV_STEPS)

                def keys_values_lo(b, p):
                    for v, dst in enumerate((kk, vT)):
                        dve.wait_ge(kv_hi, 2 * b + v + 1)
                        hi, lo = (dst[:, p, q].rearrange("p t n -> p (t n)") for q in range(2))
                        dve.scalar_tensor_tensor(out=lo, in0=raw[:, v, :], scalar=kvscale[:, v:v + 1], in1=hi,
                                                 op0=ALU.mult, op1=ALU.subtract).then_inc(kv_lo, 1)

                def negated_max(s, t):
                    dve.wait_ge(e_done, NT * s.g + t + 1)
                    dve.tensor_reduce(rowmax[:, t:t + 1], ebank[t][:, :], AX_X, ALU.max).then_inc(max_done, 1)
                    dve.wait_ge(max_done, NT * s.g + t + 1)
                    dve.tensor_scalar(nmax[:, t:t + 1], rowmax[:, t:t + 1], escale[:, s.p:s.p + 1], -1.0,
                                      ALU.mult, ALU.mult).then_inc(nmax_done, 1)

                def probabilities(s, t):
                    dve.wait_ge(exp_done, NT * s.g + t + 1)
                    dve.reciprocal(rinv[:, t:t + 1], rsum[:, t:t + 1]).then_inc(rinv_done, 1)
                    dve.wait_ge(rinv_done, NT * s.g + t + 1)
                    dve.tensor_scalar(prob[:, t, :], prob[:, t, :], rinv[:, t:t + 1], PS,
                                      ALU.mult, ALU.mult).then_inc(prob_done, 1)

                def softmax(s):
                    negated_max(s, 0)
                    negated_max(s, 1)
                    for t in range(NT):
                        if t + 2 < NT:
                            negated_max(s, t + 2)
                        probabilities(s, t)

                for j in range(STEPS):
                    chunk_stats(0, 0, 0, j)
                batch_stats(0, 0)
                first = step(0, 0, 0, 0)
                normalise(first)
                dve.wait_ge(wv_in, 32)
                dve.tensor_reduce(wsk_sc[:, 0:1], wsk_raw[:].rearrange("p t c -> p (t c)"), AX_X, ALU.max,
                                  apply_absolute_value=True).then_inc(wsk_max, 1)
                dve.wait_ge(wsk_all, 1)
                dve.tensor_scalar(wsk_sc[:, 2:3], wsk_sc[:, 1:2], TINY, None, ALU.max).then_inc(wsk_step, 1)
                dve.wait_ge(wsk_step, 1)
                dve.tensor_scalar(wsk_sc[:, 3:4].bitcast(U32), wsk_sc[:, 2:3].bitcast(U32), EXPONENT, None,
                                  ALU.bitwise_and).then_inc(wsk_step, 1)
                dve.wait_ge(wsk_step, 2)
                dve.tensor_scalar(wsk_sc[:, 4:5], wsk_sc[:, 3:4], 1.0 / TOP, None, ALU.mult).then_inc(wsk_step, 1)
                dve.wait_ge(wsk_step, 3)
                dve.tensor_scalar(wsk_sc[:, 6:7], wsk_sc[:, 4:5], 1.0 / XS, None, ALU.mult).then_inc(wsk_lo, 1)
                dve.reciprocal(wsk_sc[:, 5:6], wsk_sc[:, 4:5]).then_inc(wsk_step, 1)
                normalise(after(first))
                dve.wait_ge(wsk_hi, 1)
                dve.scalar_tensor_tensor(out=wsk[:, 1].rearrange("p t c -> p (t c)"),
                                         in0=wsk_raw[:].rearrange("p t c -> p (t c)"), scalar=wsk_sc[:, 5:6],
                                         in1=wsk[:, 0].rearrange("p t c -> p (t c)"),
                                         op0=ALU.mult, op1=ALU.subtract).then_inc(wsk_lo, 1)
                keys_values_amax(0)
                keys_values_scales(0, 0)
                keys_values_lo(0, 0)
                dve.wait_ge(lora_in, 32)
                dve.tensor_scalar(lora_b_sb[:], lora_b_sb[:], coef[:, 0:1], LORA_SCALE,
                                  ALU.mult, ALU.mult).then_inc(lora_b_ok, 1)
                softmax(first)

                def body(s, ahead):
                    last = ahead == 0
                    cols = slice(s.j * NC, (s.j + 1) * NC)
                    for t in range(NT):
                        dve.wait_ge(pT_hi, NT * s.g + t + 1)
                        dve.tensor_tensor(pT[:, 1, :, t * P:(t + 1) * P],
                                          ebank[t][:, :].rearrange("p (m n) -> p m n", m=MT),
                                          pT[:, 0, :, t * P:(t + 1) * P], ALU.subtract).then_inc(pT_lo, 1)
                    if ahead and s.j == 3:
                        keys_values_lo(s.b + 1, 1 - s.p)
                    if not (last and s.j >= 2):
                        dve.wait_ge(skip_done, CT * (s.g + 1))
                        normalise(after(s, 2))
                    if not (last and s.j == 3):
                        softmax(after(s))
                    if ahead and s.j < 2:
                        for j in (2 * s.j, 2 * s.j + 1):
                            chunk_stats(s.b + 1, s.h + s.p, 1 - s.p, j)
                    if ahead and s.j == 1:
                        batch_stats(s.b + 1, 1 - s.p)
                        keys_values_amax(s.b + 1)
                    for t in range(CT):
                        dve.wait_ge(att_done, CT * s.g + t + 1)
                        dve.wait_ge(x1a, CT * s.g + t + 1)
                        dve.scalar_tensor_tensor(out=xbuf[s.p][:, t, cols], in0=abank[t][:, :],
                                                 scalar=vscale[:, s.p:s.p + 1], in1=xbuf[s.p][:, t, cols],
                                                 op0=ALU.mult, op1=ALU.add).then_inc(x1b, 1)
                    if ahead and s.j == 1:
                        keys_values_scales(s.b + 1, 1 - s.p)

                batches(dve, body)

            @block.tensor
            def _(pe):
                def three_passes(dst, lhs, rhs, k, n):
                    pe.matmul(dst, lhs[0], rhs[0], start=(k == 0), stop=False)
                    pe.matmul(dst, lhs[0], rhs[1], start=False, stop=False)
                    return pe.matmul(dst, lhs[1], rhs[0], start=False, stop=(k == n - 1))

                def keys(b):
                    pe.wait_ge(ctx_in, 16 * (b + 1))
                    for t in range(CT):
                        for k in range(CT):
                            mm = pe.matmul(sbank[t][:, :], mT[:, k, t * P:(t + 1) * P], ctx_sb[:, k, :],
                                           start=(k == 0), stop=(k == CT - 1))
                    mm.then_inc(kk_done, 1)

                def values(b):
                    for m in range(MT):
                        for k in range(CT):
                            mm = pe.matmul(abank[m // 2][:, (m % 2) * C:(m % 2 + 1) * C],
                                           ctx_sb[:, k, m * P:(m + 1) * P], wv_sb[:, k, :],
                                           start=(k == 0), stop=(k == CT - 1))
                    mm.then_inc(v_done, 1)

                def energies(s, first=False):
                    pe.wait_ge(xn_lo, CT * (s.g + 1))
                    pe.wait_ge(kv_lo, 2 * s.b + 1)
                    for t in range(NT):
                        if not first:
                            pe.wait_ge(pT_lo, NT * (s.g - 1) + t + 1)
                        for k in range(CT):
                            mm = three_passes(ebank[t][:, :],
                                              [xn[:, s.j % 2, q, k, t * P:(t + 1) * P] for q in range(2)],
                                              [kk[:, s.p, q, k, :] for q in range(2)], k, CT)
                        mm.then_inc(e_done, 1)

                pe.wait_ge(w_in, 32)
                for t in range(CT):
                    for k in range(CT):
                        mm = pe.matmul(sbank[t][:, 0:C], qk_w[:, 1, k, t * P:(t + 1) * P], qk_w[:, 0, k, :],
                                       start=(k == 0), stop=(k == CT - 1))
                    mm.then_inc(mT_done, 1)
                pe.wait_ge(mT_ok, 1)
                pe.wait_ge(wv_in, 32)
                keys(0)
                values(0)
                first = step(0, 0, 0, 0)
                energies(first, True)
                pe.wait_ge(ident_ok, 1)
                pe.wait_ge(wsk_lo, 2)

                def body(s, ahead):
                    for t in range(NT):
                        pe.wait_ge(prob_done, NT * s.g + t + 1)
                        for m in range(MT):
                            mm = pe.transpose(ebank[t][:, m * P:(m + 1) * P], prob[:, t, m * P:(m + 1) * P], ident[:])
                        mm.then_inc(t_done, 1)
                    if s.j == 1:
                        pe.wait_ge(kk_raw, s.b + 1 + (ahead > 0))
                    for t in range(CT):
                        for k in range(CT):
                            mm = three_passes(sbank[t][:, :],
                                              [wsk[:, q, k, t * P:(t + 1) * P] for q in range(2)],
                                              [xn[:, s.j % 2, q, k, :] for q in range(2)], k, CT)
                        mm.then_inc(skip_done, 1)
                    if ahead or s.j < 3:
                        energies(after(s))
                    pe.wait_ge(pT_lo, NT * (s.g + 1))
                    pe.wait_ge(kv_lo, 2 * s.b + 2)
                    if s.j == 1:
                        pe.wait_ge(v_raw, s.b + 1 + (ahead > 0))
                    for t in range(CT):
                        for m in range(MT):
                            mm = three_passes(abank[t][:, :],
                                              [vT[:, s.p, q, m, t * P:(t + 1) * P] for q in range(2)],
                                              [pT[:, q, m, :] for q in range(2)], m, MT)
                        mm.then_inc(att_done, 1)
                    if ahead and s.j == 0:
                        pe.wait_ge(skip_out, CT * (s.g + 1))
                        keys(s.b + 1)
                        pe.wait_ge(x1b, CT * (s.g + 1))
                        values(s.b + 1)

                batches(pe, body)

        with ExitStack() as w:
            stage = sb("stage", [P, 2, N], F32, w)
            lora_a_sb = sb("lora_a_sb", [P, 2, P], F32, w)
            wrow = sb("wrow", [P, 2, 4], F32, w)
            stage_in = [sem(f"stage_in{u}") for u in range(2)]
            lora_done, lora_added = sem("lora_done"), sem("lora_added")
            wrow_step, w_hi, w_lo = sem("wrow_step"), sem("w_hi"), sem("w_lo")
            W_STEPS = 5
            block = w.enter_context(nc.Block())

            def tiles(eng, body):
                with eng.Fori(0, KT // 2) as i:
                    for u in range(2):
                        body(2 * i + u, i, u)

            @block.sync
            def _(sp):
                def load(kt, u):
                    sp.dma_start(stage[:, u, :], wT[kt]).then_inc(stage_in[u], 16)
                    sp.dma_start(lora_a_sb[:, u, :], lora_a[:, bass.ts(kt, P)]).then_inc(stage_in[u], 16)

                load(0, 0)
                load(1, 1)
                with sp.Fori(0, KT // 2 - 1) as i:
                    for u in range(2):
                        sp.wait_ge(w_lo, 2 * i + u + 1)
                        load(2 * i + u + 2, u)

            @block.tensor
            def _(pe):
                pe.wait_ge(skip_out, CT * STEPS * B)
                pe.wait_ge(x1b, CT * STEPS * B)

                def body(kt, i, u):
                    pe.wait_ge(stage_in[u], 32 * (i + 1))
                    for o in range(OC):
                        pe.matmul(bank[4 * u + o][:, :], lora_a_sb[:, u, :], lora_b_sb[:, o * NC:(o + 1) * NC],
                                  start=True, stop=True).then_inc(lora_done, 1)
                tiles(pe, body)

            @block.vector
            def _(dve):
                def body(kt, i, u):
                    dve.wait_ge(stage_in[u], 32 * (i + 1))
                    for o in range(OC):
                        dve.wait_ge(lora_done, OC * kt + o + 1)
                        cols = slice(o * NC, (o + 1) * NC)
                        dve.tensor_tensor(stage[:, u, cols], bank[4 * u + o][:, :], stage[:, u, cols],
                                          ALU.add).then_inc(lora_added, 1)
                    k = W_STEPS * kt
                    dve.wait_ge(lora_added, OC * (kt + 1))
                    dve.tensor_reduce(wrow[:, u, 0:1], stage[:, u, :], AX_X, ALU.max,
                                      apply_absolute_value=True).then_inc(wrow_step, 1)
                    dve.wait_ge(wrow_step, k + 1)
                    dve.tensor_scalar(wrow[:, u, 1:2], wrow[:, u, 0:1], TINY, None, ALU.max).then_inc(wrow_step, 1)
                    dve.wait_ge(wrow_step, k + 2)
                    dve.tensor_scalar(wmax[:, bass.ds(kt, 1)].bitcast(U32), wrow[:, u, 1:2].bitcast(U32), EXPONENT,
                                      None, ALU.bitwise_and).then_inc(wrow_step, 1)
                    dve.wait_ge(wrow_step, k + 3)
                    dve.tensor_scalar(wrow[:, u, 2:3], wmax[:, bass.ds(kt, 1)], 1.0 / TOP, None,
                                      ALU.mult).then_inc(wrow_step, 1)
                    dve.wait_ge(wrow_step, k + 4)
                    dve.reciprocal(wrow[:, u, 3:4], wrow[:, u, 2:3]).then_inc(wrow_step, 1)
                    dve.wait_ge(w_hi, kt + 1)
                    dve.scalar_tensor_tensor(out=W[:, bass.ds(kt, 1), 1, :].rearrange("p k n -> p (k n)"),
                                             in0=stage[:, u, :], scalar=wrow[:, u, 3:4],
                                             in1=W[:, bass.ds(kt, 1), 0, :].rearrange("p k n -> p (k n)"),
                                             op0=ALU.mult, op1=ALU.subtract).then_inc(w_lo, 1)
                tiles(dve, body)

            @block.scalar
            def _(act):
                def body(kt, i, u):
                    act.wait_ge(wrow_step, W_STEPS * (kt + 1))
                    act.activation(W[:, bass.ds(kt, 1), 0, :].rearrange("p k n -> p (k n)"), stage[:, u, :],
                                   ACT.Copy, scale=wrow[:, u, 3:4]).then_inc(w_hi, 1)
                tiles(act, body)

        with ExitStack() as f:
            xt = sb("xt", [P, 2, N], F32, f)
            yn = sb("yn", [P, N], F32, f)
            yT = sb("yT", [P, 2, 2, KT, P], F16, f)
            bias_sb = sb("bias_sb", [P, N], F32, f)
            stats = sb("stats2", [P, OC, 6], F32, f)
            mv = sb("mv2", [P, 2], F32, f)
            veps = sb("veps2", [P, 1], F32, f)
            half = sb("half2", [P, 1], F32, f)
            rstd = sb("rstd2", [P, 1], F32, f)
            fold = sb("fold", [P, KT], F32, f)
            top = sb("top", [P, 4], F32, f)
            mbank, tbank = bank[0:4], bank[4:8]

            xt_in = [sem(f"xt_in{u}") for u in range(2)]
            bias_in = sem("bias_in")
            out_done = sem("out_done")
            half_ok, top_max, top_all, top_step = (sem(n) for n in ("half2_ok", "top_max", "top_all", "top_step"))
            fold_ok = sem("fold_ok")
            bn_done, mv_done, veps_done, rstd_done = (sem(n) for n in ("bn2", "mv2_done", "veps2_done", "rstd2_done"))
            yn_done, biased = sem("yn_done"), sem("biased")
            t_done, y_hi, y_lo = sem("t2_done"), sem("y_hi"), sem("y_lo")
            mm_done, result = sem("mm_done"), sem("result")
            x1_r = x1.rearrange("b (t p) n -> (b t) p n", p=P)
            out_r = out.rearrange("b (t p) n -> (b t) p n", p=P)
            HALF = N // 2
            block = f.enter_context(nc.Block())

            def rows(eng, body):
                with eng.Fori(0, ROWS // 2 - 1) as i:
                    for u in range(2):
                        body(2 * i + u, i, u, 2)
                for u in range(2):
                    body(ROWS - 2 + u, ROWS // 2 - 1, u, 1 - u)

            @block.sync
            def _(sp):
                sp.wait_ge(w_lo, KT)
                sp.dma_start(xt[:, 0, :], x1_r[0]).then_inc(xt_in[0], 16)
                sp.dma_start(xt[:, 1, :], x1_r[1]).then_inc(xt_in[1], 16)
                sp.dma_start(bias_sb[:], bias.partition_broadcast(P)).then_inc(bias_in, 16)

                def body(r, i, u, ahead):
                    for q in range(2):
                        sp.wait_ge(result, OC * r + 2 * (q + 1))
                        sp.dma_start(out_r[r][:, q * HALF:(q + 1) * HALF],
                                     xt[:, u, q * HALF:(q + 1) * HALF]).then_inc(out_done, 16)
                    sp.wait_ge(out_done, 32 * (r + 1))
                    if ahead == 2:
                        sp.dma_start(xt[:, u, :], x1_r[r + 2]).then_inc(xt_in[u], 16)

                rows(sp, body)

            @block.gpsimd
            def _(pool):
                pool.wait_ge(w_lo, KT)
                pool.memset(half[:], -0.5).then_inc(half_ok, 1)
                pool.wait_ge(half_ok, 1)
                pool.wait_ge(top_max, 1)
                pool.partition_all_reduce(top[:, 1:2], top[:, 0:1], P, ABSMAX).then_inc(top_all, 1)

                def prepare(r):
                    pool.wait_ge(veps_done, r + 1)
                    pool.tensor_tensor(rstd[:], veps[:], half[:], ALU.pow).then_inc(rstd_done, 1)

                def add_bias(r, u):
                    pool.wait_ge(yn_done, r + 1)
                    pool.tensor_tensor(xt[:, u, :], xt[:, u, :], bias_sb[:], ALU.add).then_inc(biased, 1)

                prepare(0)
                pool.wait_ge(bias_in, 16)
                add_bias(0, 0)

                def body(r, i, u, ahead):
                    if ahead:
                        prepare(r + 1)
                        add_bias(r + 1, 1 - u)

                rows(pool, body)

            @block.vector
            def _(dve):
                dve.tensor_reduce(top[:, 0:1], wmax[:], AX_X, ALU.max).then_inc(top_max, 1)
                dve.wait_ge(top_all, 1)
                dve.reciprocal(top[:, 2:3], top[:, 1:2]).then_inc(top_step, 1)
                dve.tensor_scalar(top[:, 3:4], top[:, 1:2], 1.0 / (TOP * XS), None, ALU.mult).then_inc(top_step, 1)
                dve.wait_ge(top_step, 2)
                dve.tensor_scalar(fold[:], wmax[:], top[:, 2:3], None, ALU.mult).then_inc(fold_ok, 1)

                def normalise(r, i, u):
                    dve.wait_ge(xt_in[u], 16 * (i + 1))
                    for o in range(OC):
                        dve.bn_stats(stats[:, o, :], xt[:, u, o * NC:(o + 1) * NC]).then_inc(bn_done, 1)
                    dve.wait_ge(bn_done, OC * (r + 1))
                    dve.memset(carrier[:], 0.0)
                    dve.bn_aggr(mv[:], stats[:].rearrange("p o s -> p (o s)")).then_inc(mv_done, 1)
                    dve.wait_ge(mv_done, r + 1)
                    dve.tensor_scalar(veps[:], mv[:, 1:2], EPS, XS ** -2, ALU.add, ALU.mult).then_inc(veps_done, 1)
                    dve.wait_ge(rstd_done, r + 1)
                    if not (isinstance(r, int) and r == 0):
                        dve.wait_ge(t_done, 4 * r)
                    dve.tensor_scalar(yn[:], xt[:, u, :], mv[:, 0:1], rstd[:, 0:1],
                                      ALU.subtract, ALU.mult).then_inc(yn_done, 1)

                def transposed_lo(r, u):
                    for k in range(KT):
                        if k % 4 == 0:
                            dve.wait_ge(y_hi, KT * r + k + 4)
                        dve.scalar_tensor_tensor(out=yT[:, u, 1, k, :], in0=tbank[k // 4][:, (k % 4) * P:(k % 4 + 1) * P],
                                                 scalar=fold[:, k:k + 1], in1=yT[:, u, 0, k, :],
                                                 op0=ALU.mult, op1=ALU.subtract).then_inc(y_lo, 1)

                def add_product(r, u, pair):
                    for o in (2 * pair, 2 * pair + 1):
                        cols = slice(o * NC, (o + 1) * NC)
                        dve.wait_ge(mm_done, OC * r + o + 1)
                        dve.scalar_tensor_tensor(out=xt[:, u, cols], in0=mbank[o][:, :], scalar=top[:, 3:4],
                                                 in1=xt[:, u, cols], op0=ALU.mult, op1=ALU.add).then_inc(result, 1)

                normalise(0, 0, 0)
                dve.wait_ge(fold_ok, 1)
                transposed_lo(0, 0)

                def body(r, i, u, ahead):
                    if ahead:
                        normalise(r + 1, i + u, 1 - u)
                    dve.wait_ge(biased, r + 1)
                    add_product(r, u, 0)
                    if ahead:
                        transposed_lo(r + 1, 1 - u)
                    add_product(r, u, 1)

                rows(dve, body)

            @block.scalar
            def _(act):
                def transposed_hi(r, u):
                    for k in range(KT):
                        if k % 4 == 0:
                            act.wait_ge(t_done, 4 * r + k // 4 + 1)
                        act.activation(yT[:, u, 0, k, :], tbank[k // 4][:, (k % 4) * P:(k % 4 + 1) * P], ACT.Copy,
                                       scale=fold[:, k:k + 1]).then_inc(y_hi, 1)

                act.wait_ge(fold_ok, 1)
                transposed_hi(0, 0)

                def body(r, i, u, ahead):
                    if ahead:
                        transposed_hi(r + 1, 1 - u)

                rows(act, body)

            @block.tensor
            def _(pe):
                def transposes(r):
                    pe.wait_ge(yn_done, r + 1)
                    for k in range(KT):
                        mm = pe.transpose(tbank[k // 4][:, (k % 4) * P:(k % 4 + 1) * P], yn[:, k * P:(k + 1) * P], ident[:])
                        if k % 4 == 3:
                            mm.then_inc(t_done, 1)

                def products(r, u, pair):
                    cols = [slice(o * NC, (o + 1) * NC) for o in (2 * pair, 2 * pair + 1)]
                    dst = [mbank[2 * pair + q][:, :] for q in range(2)]
                    for k in range(KT):
                        hi, lo = yT[:, u, 0, k, :], yT[:, u, 1, k, :]
                        for q in range(2):
                            pe.matmul(dst[q], hi, W[:, k, 0, cols[q]], start=(k == 0), stop=False)
                        for q in range(2):
                            pe.matmul(dst[q], hi, W[:, k, 1, cols[q]], start=False, stop=False)
                        for q in range(2):
                            mm = pe.matmul(dst[q], lo, W[:, k, 0, cols[q]], start=False, stop=(k == KT - 1))
                            if k == KT - 1:
                                mm.then_inc(mm_done, 1)

                transposes(0)

                def body(r, i, u, ahead):
                    pe.wait_ge(y_lo, KT * (r + 1))
                    products(r, u, 0)
                    if ahead:
                        transposes(r + 1)
                    else:
                        pe.wait_ge(result, OC * r)
                    products(r, u, 1)

                rows(pe, body)


def kernel(x, ctx_1024, L0_xattn_Wq, L0_xattn_Wk, L0_xattn_Wv, L0_xattn_Wskip, L0_ffn_lora_A, L0_ffn_lora_B,
           L0_ffn_W, L0_ffn_bias, L0_ffn_lora_weights):
    import numpy as np
    import concourse.bacc as bacc
    from concourse.bass_utils import run_bass_kernel_spmd

    c = np.ascontiguousarray
    n_lora, rank, d_in = L0_ffn_lora_A.shape
    d_out = L0_ffn_W.shape[0]
    ins = {
        "x": c(x), "ctx": c(ctx_1024), "wq": c(L0_xattn_Wq), "wk": c(L0_xattn_Wk),
        "wvT": c(np.transpose(L0_xattn_Wv)), "wskipT": c(np.transpose(L0_xattn_Wskip)),
        "lora_a": c(np.reshape(L0_ffn_lora_A, (n_lora * rank, d_in))),
        "lora_bT": c(np.reshape(np.transpose(L0_ffn_lora_B, (0, 2, 1)), (n_lora * rank, d_out))),
        "lora_w": c(np.reshape(np.repeat(L0_ffn_lora_weights, rank), (n_lora * rank, 1))),
        "wT": c(np.reshape(np.transpose(L0_ffn_W), (d_in // P, P, d_out))),
        "bias": c(L0_ffn_bias),
    }
    nc = bacc.Bacc("TRN2", target_bir_lowering=False, num_devices=1)
    aps = [nc.dram_tensor(f"in_{k}", a.shape, mybir.dt.from_np(a.dtype), kind="ExternalInput").ap()
           for k, a in ins.items()]
    x1 = nc.dram_tensor("x1", x.shape, F32, kind="Internal").ap()
    out = nc.dram_tensor("out_x", x.shape, F32, kind="ExternalOutput").ap()
    xattn_ffn(nc, *aps, x1, out)
    r = run_bass_kernel_spmd(nc, [{f"in_{k}": a for k, a in ins.items()}], core_ids=[0])
    return r.results[0]["out_x"]
```

```python
from collections import namedtuple
from contextlib import ExitStack

import concourse.bass as bass
from concourse import mybir


P = 128
NC = 512
EPS = 1e-5
LORA_SCALE = 2.0
XS = 2.0 ** 10
PS = 2.0 ** 14
TOP = 2.0 ** 14
TINY = 2.0 ** -100

ALU = mybir.AluOpType
ACT = mybir.ActivationFunctionType
AX_X = mybir.AxisListType.X
F16 = mybir.dt.float16
F32 = mybir.dt.float32
U32 = mybir.dt.uint32
ABSMAX = bass.bass_isa.ReduceOp.absmax
EXPONENT = 0x7F800000

Step = namedtuple("Step", "g b h p j")


def xattn_ffn(nc, x, ctx_, wq, wk, wvT, wskipT, lora_a, lora_bT, lora_w, wT, bias, x1, out):
    B, C, N = x.shape
    M = ctx_.shape[2]
    R = lora_a.shape[0]
    CT, MT, KT, OC = C // P, M // P, N // P, N // NC
    STEPS = N // NC
    NT = NC // P
    ROWS = B * C // P
    assert CT == 2 and M == NC and R == P and STEPS == 4 and B % 2 == 0 and ROWS % 2 == 0

    def step(b, h, p, j):
        return Step(STEPS * b + j, b, h, p, j)

    def after(s, n=1):
        for _ in range(n):
            if s.j < STEPS - 1:
                s = Step(s.g + 1, s.b, s.h, s.p, s.j + 1)
            else:
                s = Step(s.g + 1, s.b + 1, s.h + s.p, 1 - s.p, 0)
        return s

    LOOPED = KT - 6
    LATE = {(0, 0): KT - 6, (0, 2): KT - 5, (1, 0): KT - 4, (1, 2): KT - 3}
    LEFT = (KT - 2, KT - 1)

    def batches(eng, body):
        for lo, hi, merge in ((0, LOOPED // 2, True), (LOOPED // 2, B // 2 - 1, False)):
            with eng.Fori(lo, hi) as i:
                for p in range(2):
                    for j in range(STEPS):
                        body(step(2 * i + p, i, p, j), 2, 2 * i + p if merge and j == 2 else None)
        for p in range(2):
            for j in range(STEPS):
                body(step(B - 2 + p, B // 2 - 1, p, j), 1 - p, LATE.get((p, j)))

    def merging(body):
        before = [None]

        def inner(s, ahead, merge):
            body(s, ahead, merge, before[0])
            before[0] = merge
        return inner

    with ExitStack() as stack:
        def sb(name, shape, dt, where=None):
            return (where or stack).enter_context(nc.sbuf_tensor(name, shape, dt))

        def sem(name):
            return stack.enter_context(nc.semaphore(name))

        bank = [stack.enter_context(nc.psum_tensor(f"bank{i}", [P, NC], F32)) for i in range(8)]

        W = sb("W", [P, KT, 2, N], F16)

        def spare(k0, k1):
            return W[:, k0:k1].rearrange("p k s n -> p (k s n)").bitcast(F32)

        xbuf = [spare(KT - 4 + 2 * p, KT - 2 + 2 * p).rearrange("p (t n) -> p t n", t=CT) for p in range(2)]
        raw = spare(KT - 5, KT - 4).rearrange("p (v n) -> p v n", v=2)

        ident = sb("ident", [P, P], F32)
        lora_b_sb = sb("lora_b_sb", [P, N], F32)
        coef = sb("coef", [P, 1], F32)
        carrier = sb("carrier", [P, 1], F32)
        wmax = sb("wmax", [P, KT], F32)
        wrow = sb("wrow", [P, 4], F32)

        stage_in = sem("stage_in")
        lora_done, lora_added = sem("lora_done"), sem("lora_added")
        wrow_step, w_scaled, w_hi, w_lo = sem("wrow_step"), sem("w_scaled"), sem("w_hi"), sem("w_lo")
        W_STEPS = 5

        def merge_load(sp, kt, stage, lora_a_t):
            sp.dma_start(stage, wT[kt]).then_inc(stage_in, 16)
            sp.dma_start(lora_a_t, lora_a[:, bass.ts(kt, P)]).then_inc(stage_in, 16)

        def merge_product(pe, o, lora_a_t, dst):
            pe.matmul(dst[:, :], lora_a_t, lora_b_sb[:, o * NC:(o + 1) * NC],
                      start=True, stop=True).then_inc(lora_done, 1)

        def merge_add(dve, kt, o, stage, src):
            dve.wait_ge(lora_done, OC * kt + o + 1)
            cols = slice(o * NC, (o + 1) * NC)
            dve.tensor_tensor(stage[:, cols], src[:, :], stage[:, cols], ALU.add).then_inc(lora_added, 1)

        def merge_scale(dve, kt, stage):
            k = W_STEPS * kt
            dve.wait_ge(lora_added, OC * (kt + 1))
            dve.tensor_reduce(wrow[:, 0:1], stage, AX_X, ALU.max, apply_absolute_value=True).then_inc(wrow_step, 1)
            dve.wait_ge(wrow_step, k + 1)
            dve.tensor_scalar(wrow[:, 1:2], wrow[:, 0:1], TINY, None, ALU.max).then_inc(wrow_step, 1)
            dve.wait_ge(wrow_step, k + 2)
            dve.tensor_scalar(wmax[:, bass.ds(kt, 1)].bitcast(U32), wrow[:, 1:2].bitcast(U32), EXPONENT,
                              None, ALU.bitwise_and).then_inc(wrow_step, 1)
            dve.wait_ge(wrow_step, k + 3)
            dve.tensor_scalar(wrow[:, 2:3], wmax[:, bass.ds(kt, 1)], 1.0 / TOP, None, ALU.mult).then_inc(wrow_step, 1)
            dve.wait_ge(wrow_step, k + 4)
            dve.reciprocal(wrow[:, 3:4], wrow[:, 2:3]).then_inc(wrow_step, 1)

        def half_of(kt, q):
            return W[:, bass.ds(kt, 1), q, :].rearrange("p k n -> p (k n)")

        def merge_hi(act, kt, stage):
            act.wait_ge(wrow_step, W_STEPS * (kt + 1))
            act.activation(stage, stage, ACT.Copy, scale=wrow[:, 3:4]).then_inc(w_scaled, 1)
            act.wait_ge(w_scaled, kt + 1)
            act.activation(half_of(kt, 0), stage, ACT.Copy).then_inc(w_hi, 1)

        def merge_lo(pool, kt, stage):
            pool.wait_ge(w_hi, kt + 1)
            pool.tensor_tensor(half_of(kt, 1), stage, half_of(kt, 0), ALU.subtract).then_inc(w_lo, 1)

        with ExitStack() as a:
            stage = sb("stage", [P, N], F32, a)
            qk_w = stage[:, 0:2 * CT * C].rearrange("p (w t c) -> p w t c", w=2, t=CT)
            wsk_raw = stage[:, 2 * CT * C:3 * CT * C].rearrange("p (t c) -> p t c", t=CT)
            lora_a_sb = sb("lora_a_sb", [P, P], F32, a)
            mT = sb("mT", [P, CT, C], F32, a)
            wv_sb = sb("wv_sb", [P, CT, C], F32, a)
            wsk = sb("wsk", [P, 2, CT, C], F16, a)
            ctx_sb = sb("ctx_sb", [P, CT, M], F32, a)
            xn32 = sb("xn32", [P, CT, NC], F32, a)
            xn = sb("xn", [P, 2, 2, CT, NC], F16, a)
            kk = sb("kk", [P, 2, 2, CT, M], F16, a)
            vT = sb("vT", [P, 2, 2, MT, C], F16, a)
            prob = sb("prob", [P, NT, M], F32, a)
            pT = sb("pT", [P, 2, MT, NC], F16, a)
            skip32 = sb("skip32", [P, CT, NC], F32, a)
            stats = sb("stats", [P, CT, STEPS, 6], F32, a)
            mv = sb("mv", [P, 2, CT, 2], F32, a)
            veps = sb("veps", [P, CT], F32, a)
            half = sb("half", [P, CT], F32, a)
            rstd = sb("rstd", [P, 2, CT], F32, a)
            amax = sb("amax", [P, 2], F32, a)
            gmax = sb("gmax", [P, 2], F32, a)
            cmax = sb("cmax", [P, 2], F32, a)
            pow2 = sb("pow2", [P, 2], F32, a)
            unscale = sb("unscale", [P, 2], F32, a)
            kvscale = sb("kvscale", [P, 2], F32, a)
            escale = sb("escale", [P, 2], F32, a)
            vscale = sb("vscale", [P, 2], F32, a)
            wsk_sc = sb("wsk_sc", [P, 8], F32, a)
            rowmax = sb("rowmax", [P, NT], F32, a)
            nmax = sb("nmax", [P, NT], F32, a)
            rsum = sb("rsum", [P, NT], F32, a)
            rinv = sb("rinv", [P, NT], F32, a)
            KV_STEPS = 6
            ebank, sbank, abank = bank[0:4], bank[4:6], bank[6:8]

            w_in = sem("w_in")
            wv_in = sem("wv_in")
            lora_in = sem("lora_in")
            x_in = [[sem(f"x_in{p}{j}") for j in range(STEPS)] for p in range(2)]
            ctx_in = sem("ctx_in")
            x1_out = sem("x1_out")
            ident_zero, ident_ok = sem("ident_zero"), sem("ident_ok")
            half_ok, lora_b_ok = sem("half_ok"), sem("lora_b_ok")
            mT_done, mT_ok = sem("mT_done"), sem("mT_ok")
            wsk_max, wsk_all, wsk_step = sem("wsk_max"), sem("wsk_all"), sem("wsk_step")
            wsk_hi, wsk_lo = sem("wsk_hi"), sem("wsk_lo")
            bn_done, mv_done, veps_done = sem("bn_done"), sem("mv_done"), sem("veps_done")
            rstd_done = sem("rstd_done")
            kk_done, v_done = sem("kk_done"), sem("v_done")
            kk_raw, v_raw = sem("kk_raw"), sem("v_raw")
            kv_max, kv_all, kv_step = sem("kv_max"), sem("kv_all"), sem("kv_step")
            kv_hi, kv_lo = sem("kv_hi"), sem("kv_lo")
            xn_done, xn_hi, xn_lo = sem("xn_done"), sem("xn_hi"), sem("xn_lo")
            skip_done, skip_out, x1a = sem("skip_done"), sem("skip_out"), sem("x1a")
            att_done, x1b = sem("att_done"), sem("x1b")
            e_done, max_done, nmax_done = sem("e_done"), sem("max_done"), sem("nmax_done")
            exp_done, rinv_done, prob_done = sem("exp_done"), sem("rinv_done"), sem("prob_done")
            t_done, pT_hi, pT_lo = sem("t_done"), sem("pT_hi"), sem("pT_lo")

            x_v = x.rearrange("b (t p) n -> b p t n", p=P)
            x1_v = x1.rearrange("b (t p) n -> b p t n", p=P)
            ctx_v = ctx_.rearrange("b (t p) m -> b p t m", p=P)

            block = a.enter_context(nc.Block())

            @block.sync
            def _(sp):
                for b in range(2):
                    for j in range(STEPS):
                        cols = slice(j * NC, (j + 1) * NC)
                        sp.dma_start(xbuf[b][:, :, cols], x_v[b][:, :, cols]).then_inc(x_in[b][j], 16)
                sp.wait_ge(v_done, 1)
                sp.dma_start(ctx_sb[:], ctx_v[1]).then_inc(ctx_in, 16)
                sp.wait_ge(mT_done, CT)
                sp.wait_ge(wsk_lo, 2)
                merge_load(sp, 0, stage[:], lora_a_sb[:])

                def load_next(kt):
                    sp.wait_ge(w_lo, kt)
                    merge_load(sp, kt, stage[:], lora_a_sb[:])

                def body(s, ahead, merge):
                    cols = slice(s.j * NC, (s.j + 1) * NC)
                    sp.wait_ge(x1b, CT * (s.g + 1))
                    sp.dma_start(x1_v[s.b][:, :, cols], xbuf[s.p][:, :, cols]).then_inc(x1_out, 16)
                    sp.wait_ge(x1_out, 16 * (s.g + 1))
                    if ahead == 2:
                        sp.dma_start(xbuf[s.p][:, :, cols], x_v[s.b + 2][:, :, cols]).then_inc(x_in[s.p][s.j], 16)
                        if s.j == 0:
                            sp.wait_ge(v_done, s.b + 2)
                            sp.dma_start(ctx_sb[:], ctx_v[s.b + 2]).then_inc(ctx_in, 16)
                    if merged[0] is not None and s.j == 3:
                        load_next(merged[0] + 1)
                    late = {(0, 1): KT - 5, (0, 3): KT - 4, (1, 1): KT - 3}.get((s.p, s.j))
                    if ahead < 2 and late:
                        load_next(late)
                    merged[0] = merge if ahead == 2 else None

                merged = [None]
                batches(sp, body)

            @block.scalar
            def _(act):
                act.dma_start(ctx_sb[:], ctx_v[0]).then_inc(ctx_in, 16)
                act.dma_start(qk_w[:, 0], wq.rearrange("(t p) c -> p t c", p=P)).then_inc(w_in, 16)
                act.dma_start(qk_w[:, 1], wk.rearrange("(t p) c -> p t c", p=P)).then_inc(w_in, 16)
                act.dma_start(wv_sb[:], wvT.rearrange("(t p) c -> p t c", p=P)).then_inc(wv_in, 16)
                act.dma_start(wsk_raw, wskipT.rearrange("(t p) c -> p t c", p=P)).then_inc(wv_in, 16)
                act.dma_start(lora_b_sb[:], lora_bT).then_inc(lora_in, 16)
                act.dma_start(coef[:], lora_w).then_inc(lora_in, 16)
                act.wait_ge(mT_done, CT)
                for t in range(CT):
                    last = act.activation(mT[:, t, :], sbank[t][:, 0:C], ACT.Copy)
                last.then_inc(mT_ok, 1)

                def keys_values_raw(b):
                    act.wait_ge(kk_done, b + 1)
                    for t in range(CT):
                        last = act.activation(raw[:, 0, t * M:(t + 1) * M], sbank[t][:, :], ACT.Copy)
                    last.then_inc(kk_raw, 1)
                    act.wait_ge(v_done, b + 1)
                    for t in range(2):
                        last = act.activation(raw[:, 1, t * NC:(t + 1) * NC], abank[t][:, :], ACT.Copy)
                    last.then_inc(v_raw, 1)

                def keys_values_hi(b, p):
                    act.wait_ge(kv_step, KV_STEPS * b + 4)
                    for v, dst in enumerate((kk, vT)):
                        act.activation(dst[:, p, 0].rearrange("p t n -> p (t n)"), raw[:, v, :], ACT.Copy,
                                       scale=kvscale[:, v:v + 1]).then_inc(kv_hi, 1)

                def exponentials(s):
                    for t in range(NT):
                        act.wait_ge(nmax_done, NT * s.g + t + 1)
                        act.activation(prob[:, t, :], ebank[t][:, :], ACT.Exp, bias=nmax[:, t:t + 1],
                                       scale=escale[:, s.p:s.p + 1], accum_out=rsum[:, t:t + 1]).then_inc(exp_done, 1)

                def xn_hi_of(s):
                    for t in range(CT):
                        act.wait_ge(xn_done, CT * s.g + t + 1)
                        act.activation(xn[:, s.j % 2, 0, t, :], xn32[:, t, :], ACT.Copy).then_inc(xn_hi, 1)

                first = step(0, 0, 0, 0)
                xn_hi_of(first)
                act.wait_ge(wsk_step, 4)
                act.activation(wsk[:, 0].rearrange("p t c -> p (t c)"), stage[:, 2 * CT * C:3 * CT * C],
                               ACT.Copy, scale=wsk_sc[:, 5:6]).then_inc(wsk_hi, 1)
                xn_hi_of(after(first))
                keys_values_raw(0)
                keys_values_hi(0, 0)
                exponentials(first)

                @merging
                def body(s, ahead, merge, merged):
                    for t in range(NT):
                        act.wait_ge(t_done, NT * s.g + t + 1)
                        act.activation(pT[:, 0, :, t * P:(t + 1) * P],
                                       ebank[t][:, :].rearrange("p (m n) -> p m n", m=MT), ACT.Copy).then_inc(pT_hi, 1)
                    act.wait_ge(pT_lo, NT * s.g + 1)
                    for t in range(CT):
                        act.wait_ge(skip_done, CT * s.g + t + 1)
                        act.activation(skip32[:, t, :], sbank[t][:, :], ACT.Copy,
                                       scale=wsk_sc[:, 6:7]).then_inc(skip_out, 1)
                    last = ahead == 0
                    if ahead and s.j == 2:
                        keys_values_hi(s.b + 1, 1 - s.p)
                    if not (last and s.j == 3):
                        exponentials(after(s))
                    if not (last and s.j >= 2):
                        xn_hi_of(after(s, 2))
                    if ahead and s.j == 0:
                        keys_values_raw(s.b + 1)
                    if merged is not None:
                        if isinstance(merged, int) and merged == KT - 5:
                            act.wait_ge(kv_lo, 2 * B)
                        if isinstance(merged, int) and merged == KT - 4:
                            act.wait_ge(x1_out, 16 * STEPS * (B - 1))
                        merge_hi(act, merged, stage[:])

                batches(act, body)

            @block.gpsimd
            def _(pool):
                pool.memset(ident[:], 0.0).then_inc(ident_zero, 1)
                pool.wait_ge(ident_zero, 1)
                pool.affine_select(out=ident[:], in_=ident[:], compare_op=ALU.not_equal, fill=1.0, base=0,
                                   pattern=[[-1, P]], channel_multiplier=1).then_inc(ident_ok, 1)
                pool.memset(half[:], -0.5).then_inc(half_ok, 1)
                pool.wait_ge(half_ok, 1)

                def inverse_deviation(b, p):
                    pool.wait_ge(veps_done, b + 1)
                    pool.tensor_tensor(rstd[:, p, :], veps[:], half[:], ALU.pow).then_inc(rstd_done, 1)

                def keys_values_max():
                    pool.partition_all_reduce(gmax[:], amax[:], P, ABSMAX).then_inc(kv_all, 1)

                def normalised_lo(s):
                    for t in range(CT):
                        pool.wait_ge(xn_hi, CT * s.g + t + 1)
                        pool.tensor_tensor(xn[:, s.j % 2, 1, t, :], xn32[:, t, :], xn[:, s.j % 2, 0, t, :],
                                           ALU.subtract).then_inc(xn_lo, 1)

                first = step(0, 0, 0, 0)
                inverse_deviation(0, 0)
                normalised_lo(first)
                pool.wait_ge(wsk_max, 1)
                pool.partition_all_reduce(wsk_sc[:, 1:2], wsk_sc[:, 0:1], P, ABSMAX).then_inc(wsk_all, 1)
                normalised_lo(after(first))
                pool.wait_ge(kv_max, 2)
                keys_values_max()

                @merging
                def body(s, ahead, merge, merged):
                    last = ahead == 0
                    cols = slice(s.j * NC, (s.j + 1) * NC)
                    for t in range(CT):
                        pool.wait_ge(skip_out, CT * s.g + t + 1)
                        pool.tensor_tensor(xbuf[s.p][:, t, cols], xbuf[s.p][:, t, cols], skip32[:, t, :],
                                           ALU.add).then_inc(x1a, 1)
                    if not (last and s.j >= 2):
                        normalised_lo(after(s, 2))
                    if ahead and s.j == 1:
                        pool.wait_ge(kv_max, 2 * (s.b + 2))
                        inverse_deviation(s.b + 1, 1 - s.p)
                        keys_values_max()
                    if merged is not None:
                        merge_lo(pool, merged, stage[:])

                batches(pool, body)

            @block.vector
            def _(dve):
                def chunk_stats(b, h, p, j):
                    dve.wait_ge(x_in[p][j], 16 * (h + 1))
                    for t in range(CT):
                        dve.bn_stats(stats[:, t, j, :], xbuf[p][:, t, j * NC:(j + 1) * NC]).then_inc(bn_done, 1)

                def batch_stats(b, p):
                    dve.wait_ge(bn_done, CT * STEPS * (b + 1))
                    dve.memset(carrier[:], 0.0)
                    for t in range(CT):
                        dve.bn_aggr(mv[:, p, t, :], stats[:, t].rearrange("p j s -> p (j s)")).then_inc(mv_done, 1)
                    dve.wait_ge(mv_done, CT * (b + 1))
                    dve.tensor_scalar(veps[:], mv[:, p, :, 1], EPS, XS ** -2, ALU.add, ALU.mult).then_inc(veps_done, 1)

                def normalise(s):
                    dve.wait_ge(rstd_done, s.b + 1)
                    dve.wait_ge(xn_lo, CT * s.g)
                    for t in range(CT):
                        dve.tensor_scalar(xn32[:, t, :], xbuf[s.p][:, t, s.j * NC:(s.j + 1) * NC],
                                          mv[:, s.p, t, 0:1], rstd[:, s.p, t:t + 1],
                                          ALU.subtract, ALU.mult).then_inc(xn_done, 1)

                def keys_values_amax(b):
                    for v, ready in enumerate((kk_raw, v_raw)):
                        dve.wait_ge(ready, b + 1)
                        dve.tensor_reduce(amax[:, v:v + 1], raw[:, v, :], AX_X, ALU.max,
                                          apply_absolute_value=True).then_inc(kv_max, 1)

                def keys_values_scales(b, p):
                    k = KV_STEPS * b
                    dve.wait_ge(kv_all, b + 1)
                    dve.tensor_scalar(cmax[:], gmax[:], TINY, None, ALU.max).then_inc(kv_step, 1)
                    dve.wait_ge(kv_step, k + 1)
                    dve.tensor_scalar(pow2[:].bitcast(U32), cmax[:].bitcast(U32), EXPONENT, None,
                                      ALU.bitwise_and).then_inc(kv_step, 1)
                    dve.wait_ge(kv_step, k + 2)
                    dve.tensor_scalar(unscale[:], pow2[:], 1.0 / TOP, None, ALU.mult).then_inc(kv_step, 1)
                    dve.wait_ge(kv_step, k + 3)
                    dve.reciprocal(kvscale[:], unscale[:]).then_inc(kv_step, 1)
                    dve.tensor_scalar(escale[:, p:p + 1], unscale[:, 0:1], 1.0 / (XS * C ** 0.5), None,
                                      ALU.mult).then_inc(kv_step, 1)
                    dve.tensor_scalar(vscale[:, p:p + 1], unscale[:, 1:2], 1.0 / PS, None,
                                      ALU.mult).then_inc(kv_step, 1)
                    dve.wait_ge(kv_step, k + KV_STEPS)

                def keys_values_lo(b, p, v):
                    dve.wait_ge(kv_hi, 2 * b + v + 1)
                    hi, lo = ((kk, vT)[v][:, p, q].rearrange("p t n -> p (t n)") for q in range(2))
                    dve.scalar_tensor_tensor(out=lo, in0=raw[:, v, :], scalar=kvscale[:, v:v + 1], in1=hi,
                                             op0=ALU.mult, op1=ALU.subtract).then_inc(kv_lo, 1)

                def negated_max(s, t):
                    dve.wait_ge(e_done, NT * s.g + t + 1)
                    dve.tensor_reduce(rowmax[:, t:t + 1], ebank[t][:, :], AX_X, ALU.max).then_inc(max_done, 1)
                    dve.wait_ge(max_done, NT * s.g + t + 1)
                    dve.tensor_scalar(nmax[:, t:t + 1], rowmax[:, t:t + 1], escale[:, s.p:s.p + 1], -1.0,
                                      ALU.mult, ALU.mult).then_inc(nmax_done, 1)

                def probabilities(s, t):
                    dve.wait_ge(exp_done, NT * s.g + t + 1)
                    dve.reciprocal(rinv[:, t:t + 1], rsum[:, t:t + 1]).then_inc(rinv_done, 1)
                    dve.wait_ge(rinv_done, NT * s.g + t + 1)
                    dve.tensor_scalar(prob[:, t, :], prob[:, t, :], rinv[:, t:t + 1], PS,
                                      ALU.mult, ALU.mult).then_inc(prob_done, 1)

                def softmax(s):
                    negated_max(s, 0)
                    negated_max(s, 1)
                    for t in range(NT):
                        if t + 2 < NT:
                            negated_max(s, t + 2)
                        probabilities(s, t)

                for j in range(STEPS):
                    chunk_stats(0, 0, 0, j)
                batch_stats(0, 0)
                first = step(0, 0, 0, 0)
                normalise(first)
                dve.wait_ge(wv_in, 32)
                dve.tensor_reduce(wsk_sc[:, 0:1], stage[:, 2 * CT * C:3 * CT * C], AX_X, ALU.max,
                                  apply_absolute_value=True).then_inc(wsk_max, 1)
                dve.wait_ge(wsk_all, 1)
                dve.tensor_scalar(wsk_sc[:, 2:3], wsk_sc[:, 1:2], TINY, None, ALU.max).then_inc(wsk_step, 1)
                dve.wait_ge(wsk_step, 1)
                dve.tensor_scalar(wsk_sc[:, 3:4].bitcast(U32), wsk_sc[:, 2:3].bitcast(U32), EXPONENT, None,
                                  ALU.bitwise_and).then_inc(wsk_step, 1)
                dve.wait_ge(wsk_step, 2)
                dve.tensor_scalar(wsk_sc[:, 4:5], wsk_sc[:, 3:4], 1.0 / TOP, None, ALU.mult).then_inc(wsk_step, 1)
                dve.wait_ge(wsk_step, 3)
                dve.tensor_scalar(wsk_sc[:, 6:7], wsk_sc[:, 4:5], 1.0 / XS, None, ALU.mult).then_inc(wsk_lo, 1)
                dve.reciprocal(wsk_sc[:, 5:6], wsk_sc[:, 4:5]).then_inc(wsk_step, 1)
                normalise(after(first))
                dve.wait_ge(wsk_hi, 1)
                dve.scalar_tensor_tensor(out=wsk[:, 1].rearrange("p t c -> p (t c)"),
                                         in0=stage[:, 2 * CT * C:3 * CT * C], scalar=wsk_sc[:, 5:6],
                                         in1=wsk[:, 0].rearrange("p t c -> p (t c)"),
                                         op0=ALU.mult, op1=ALU.subtract).then_inc(wsk_lo, 1)
                keys_values_amax(0)
                keys_values_scales(0, 0)
                keys_values_lo(0, 0, 0)
                keys_values_lo(0, 0, 1)
                dve.wait_ge(lora_in, 32)
                dve.tensor_scalar(lora_b_sb[:], lora_b_sb[:], coef[:, 0:1], LORA_SCALE,
                                  ALU.mult, ALU.mult).then_inc(lora_b_ok, 1)
                softmax(first)

                @merging
                def body(s, ahead, merge, merged):
                    last = ahead == 0
                    cols = slice(s.j * NC, (s.j + 1) * NC)
                    for t in range(NT):
                        dve.wait_ge(pT_hi, NT * s.g + t + 1)
                        dve.tensor_tensor(pT[:, 1, :, t * P:(t + 1) * P],
                                          ebank[t][:, :].rearrange("p (m n) -> p m n", m=MT),
                                          pT[:, 0, :, t * P:(t + 1) * P], ALU.subtract).then_inc(pT_lo, 1)
                    if ahead and s.j == 3:
                        keys_values_lo(s.b + 1, 1 - s.p, 0)
                    if not (last and s.j >= 2):
                        dve.wait_ge(skip_done, CT * (s.g + 1))
                        normalise(after(s, 2))
                    if ahead and s.j == 0:
                        for j in range(2):
                            chunk_stats(s.b + 1, s.h + s.p, 1 - s.p, j)
                    if ahead and s.j == 1:
                        keys_values_amax(s.b + 1)
                    if merged is not None:
                        merge_scale(dve, merged, stage[:])
                    if not (last and s.j == 3):
                        softmax(after(s))
                    if ahead and s.j == 0:
                        for j in range(2, STEPS):
                            chunk_stats(s.b + 1, s.h + s.p, 1 - s.p, j)
                    if ahead and s.j == 1:
                        batch_stats(s.b + 1, 1 - s.p)
                    if ahead and s.j == 3:
                        keys_values_lo(s.b + 1, 1 - s.p, 1)
                    for t in range(CT):
                        dve.wait_ge(att_done, CT * s.g + t + 1)
                        dve.wait_ge(x1a, CT * s.g + t + 1)
                        dve.scalar_tensor_tensor(out=xbuf[s.p][:, t, cols], in0=abank[t][:, :],
                                                 scalar=vscale[:, s.p:s.p + 1], in1=xbuf[s.p][:, t, cols],
                                                 op0=ALU.mult, op1=ALU.add).then_inc(x1b, 1)
                    if ahead and s.j == 1:
                        keys_values_scales(s.b + 1, 1 - s.p)
                    if merge is not None:
                        for o in range(OC):
                            merge_add(dve, merge, o, stage[:], bank[4 + o])

                batches(dve, body)

            @block.tensor
            def _(pe):
                def three_passes(dst, lhs, rhs, k, n):
                    pe.matmul(dst, lhs[0], rhs[0], start=(k == 0), stop=False)
                    pe.matmul(dst, lhs[0], rhs[1], start=False, stop=False)
                    return pe.matmul(dst, lhs[1], rhs[0], start=False, stop=(k == n - 1))

                def keys(b):
                    pe.wait_ge(ctx_in, 16 * (b + 1))
                    for t in range(CT):
                        for k in range(CT):
                            mm = pe.matmul(sbank[t][:, :], mT[:, k, t * P:(t + 1) * P], ctx_sb[:, k, :],
                                           start=(k == 0), stop=(k == CT - 1))
                    mm.then_inc(kk_done, 1)

                def values(b):
                    for m in range(MT):
                        for k in range(CT):
                            mm = pe.matmul(abank[m // 2][:, (m % 2) * C:(m % 2 + 1) * C],
                                           ctx_sb[:, k, m * P:(m + 1) * P], wv_sb[:, k, :],
                                           start=(k == 0), stop=(k == CT - 1))
                    mm.then_inc(v_done, 1)

                def energies(s, first=False):
                    pe.wait_ge(xn_lo, CT * (s.g + 1))
                    pe.wait_ge(kv_lo, 2 * s.b + 1)
                    for t in range(NT):
                        if not first:
                            pe.wait_ge(pT_lo, NT * (s.g - 1) + t + 1)
                        for k in range(CT):
                            mm = three_passes(ebank[t][:, :],
                                              [xn[:, s.j % 2, q, k, t * P:(t + 1) * P] for q in range(2)],
                                              [kk[:, s.p, q, k, :] for q in range(2)], k, CT)
                        mm.then_inc(e_done, 1)

                pe.wait_ge(w_in, 32)
                for t in range(CT):
                    for k in range(CT):
                        mm = pe.matmul(sbank[t][:, 0:C], qk_w[:, 1, k, t * P:(t + 1) * P], qk_w[:, 0, k, :],
                                       start=(k == 0), stop=(k == CT - 1))
                    mm.then_inc(mT_done, 1)
                pe.wait_ge(mT_ok, 1)
                pe.wait_ge(wv_in, 32)
                keys(0)
                values(0)
                first = step(0, 0, 0, 0)
                energies(first, True)
                pe.wait_ge(ident_ok, 1)
                pe.wait_ge(wsk_lo, 2)
                pe.wait_ge(lora_b_ok, 1)

                @merging
                def body(s, ahead, merge, merged):
                    for t in range(NT):
                        pe.wait_ge(prob_done, NT * s.g + t + 1)
                        for m in range(MT):
                            mm = pe.transpose(ebank[t][:, m * P:(m + 1) * P], prob[:, t, m * P:(m + 1) * P], ident[:])
                        mm.then_inc(t_done, 1)
                    if s.j == 1:
                        pe.wait_ge(kk_raw, s.b + 1 + (ahead > 0))
                    if merged is not None:
                        pe.wait_ge(lora_added, OC * merged + 2)
                    for t in range(CT):
                        for k in range(CT):
                            mm = three_passes(sbank[t][:, :],
                                              [wsk[:, q, k, t * P:(t + 1) * P] for q in range(2)],
                                              [xn[:, s.j % 2, q, k, :] for q in range(2)], k, CT)
                        mm.then_inc(skip_done, 1)
                    if ahead or s.j < 3:
                        energies(after(s))
                    pe.wait_ge(pT_lo, NT * (s.g + 1))
                    pe.wait_ge(kv_lo, 2 * s.b + 2)
                    if s.j == 1:
                        pe.wait_ge(v_raw, s.b + 1 + (ahead > 0))
                    for t in range(CT):
                        for m in range(MT):
                            mm = three_passes(abank[t][:, :],
                                              [vT[:, s.p, q, m, t * P:(t + 1) * P] for q in range(2)],
                                              [pT[:, q, m, :] for q in range(2)], m, MT)
                        mm.then_inc(att_done, 1)
                    if ahead and s.j == 0:
                        pe.wait_ge(skip_out, CT * (s.g + 1))
                        keys(s.b + 1)
                        pe.wait_ge(x1b, CT * (s.g + 1))
                        values(s.b + 1)
                    if merge is not None:
                        pe.wait_ge(stage_in, 32 * (merge + 1))
                        pe.wait_ge(skip_out, CT * (s.g + 1))
                        if ahead and s.j == 0:
                            pe.wait_ge(kk_raw, s.b + 2)
                        for o in range(OC):
                            if o == 2:
                                pe.wait_ge(x1b, CT * (s.g + 1))
                                if ahead and s.j == 0:
                                    pe.wait_ge(v_raw, s.b + 2)
                            merge_product(pe, o, lora_a_sb[:], bank[4 + o])

                batches(pe, body)

        with ExitStack() as f:
            xt = sb("xt", [P, 2, N], F32, f)
            yn = sb("yn", [P, N], F32, f)
            yT = sb("yT", [P, 2, 2, KT, P], F16, f)
            bias_sb = sb("bias_sb", [P, N], F32, f)
            stages = sb("stages", [P, 2, N], F32, f)
            lora_as = sb("lora_as", [P, 2, P], F32, f)
            stats = sb("stats2", [P, OC, 6], F32, f)
            mv = sb("mv2", [P, 2], F32, f)
            veps = sb("veps2", [P, 1], F32, f)
            half = sb("half2", [P, 1], F32, f)
            rstd = sb("rstd2", [P, 1], F32, f)
            fold = sb("fold", [P, KT], F32, f)
            top = sb("top", [P, 4], F32, f)
            mbank, tbank = bank[0:4], bank[4:8]

            xt_in = [sem(f"xt_in{u}") for u in range(2)]
            bias_in = sem("bias_in")
            out_done = sem("out_done")
            half_ok, top_max, top_all, top_step = (sem(n) for n in ("half2_ok", "top_max", "top_all", "top_step"))
            fold_ok = sem("fold_ok")
            bn_done, mv_done, veps_done, rstd_done = (sem(n) for n in ("bn2", "mv2_done", "veps2_done", "rstd2_done"))
            yn_done, biased = sem("yn_done"), sem("biased")
            t_done, y_hi, y_lo = sem("t2_done"), sem("y_hi"), sem("y_lo")
            mm_done, result = sem("mm_done"), sem("result")
            x1_r = x1.rearrange("b (t p) n -> (b t) p n", p=P)
            out_r = out.rearrange("b (t p) n -> (b t) p n", p=P)
            HALF = N // 2
            block = f.enter_context(nc.Block())

            def rows(eng, body):
                with eng.Fori(0, ROWS // 2 - 1) as i:
                    for u in range(2):
                        body(2 * i + u, i, u, 2)
                for u in range(2):
                    body(ROWS - 2 + u, ROWS // 2 - 1, u, 1 - u)

            @block.sync
            def _(sp):
                sp.wait_ge(w_lo, LEFT[0])
                for n, kt in enumerate(LEFT):
                    merge_load(sp, kt, stages[:, n, :], lora_as[:, n, :])
                sp.dma_start(xt[:, 0, :], x1_r[0]).then_inc(xt_in[0], 16)
                sp.dma_start(xt[:, 1, :], x1_r[1]).then_inc(xt_in[1], 16)
                sp.dma_start(bias_sb[:], bias.partition_broadcast(P)).then_inc(bias_in, 16)

                def body(r, i, u, ahead):
                    for q in range(2):
                        sp.wait_ge(result, OC * r + 2 * (q + 1))
                        sp.dma_start(out_r[r][:, q * HALF:(q + 1) * HALF],
                                     xt[:, u, q * HALF:(q + 1) * HALF]).then_inc(out_done, 16)
                    sp.wait_ge(out_done, 32 * (r + 1))
                    if ahead == 2:
                        sp.dma_start(xt[:, u, :], x1_r[r + 2]).then_inc(xt_in[u], 16)

                rows(sp, body)

            @block.gpsimd
            def _(pool):
                def prepare(r):
                    pool.wait_ge(veps_done, r + 1)
                    pool.tensor_tensor(rstd[:], veps[:], half[:], ALU.pow).then_inc(rstd_done, 1)

                pool.wait_ge(x1b, CT * STEPS * B)
                pool.memset(half[:], -0.5).then_inc(half_ok, 1)
                pool.wait_ge(half_ok, 1)
                prepare(0)
                pool.wait_ge(top_max, 1)
                pool.partition_all_reduce(top[:, 1:2], top[:, 0:1], P, ABSMAX).then_inc(top_all, 1)

                def add_bias(r, u):
                    pool.wait_ge(yn_done, r + 1)
                    pool.tensor_tensor(xt[:, u, :], xt[:, u, :], bias_sb[:], ALU.add).then_inc(biased, 1)

                for n, kt in enumerate(LEFT):
                    merge_lo(pool, kt, stages[:, n, :])
                pool.wait_ge(bias_in, 16)
                add_bias(0, 0)

                def body(r, i, u, ahead):
                    if ahead:
                        prepare(r + 1)
                        add_bias(r + 1, 1 - u)

                rows(pool, body)

            @block.vector
            def _(dve):
                def normalise(r, i, u):
                    dve.wait_ge(xt_in[u], 16 * (i + 1))
                    for o in range(OC):
                        dve.bn_stats(stats[:, o, :], xt[:, u, o * NC:(o + 1) * NC]).then_inc(bn_done, 1)
                    dve.wait_ge(bn_done, OC * (r + 1))
                    dve.memset(carrier[:], 0.0)
                    dve.bn_aggr(mv[:], stats[:].rearrange("p o s -> p (o s)")).then_inc(mv_done, 1)
                    dve.wait_ge(mv_done, r + 1)
                    dve.tensor_scalar(veps[:], mv[:, 1:2], EPS, XS ** -2, ALU.add, ALU.mult).then_inc(veps_done, 1)
                    dve.wait_ge(rstd_done, r + 1)
                    if not (isinstance(r, int) and r == 0):
                        dve.wait_ge(t_done, 4 * r)
                    dve.tensor_scalar(yn[:], xt[:, u, :], mv[:, 0:1], rstd[:, 0:1],
                                      ALU.subtract, ALU.mult).then_inc(yn_done, 1)

                def transposed_lo(r, u):
                    for k in range(KT):
                        if k % 4 == 0:
                            dve.wait_ge(y_hi, KT * r + k + 4)
                        dve.scalar_tensor_tensor(out=yT[:, u, 1, k, :], in0=tbank[k // 4][:, (k % 4) * P:(k % 4 + 1) * P],
                                                 scalar=fold[:, k:k + 1], in1=yT[:, u, 0, k, :],
                                                 op0=ALU.mult, op1=ALU.subtract).then_inc(y_lo, 1)

                def add_product(r, u, pair):
                    for o in (2 * pair, 2 * pair + 1):
                        cols = slice(o * NC, (o + 1) * NC)
                        dve.wait_ge(mm_done, OC * r + o + 1)
                        dve.scalar_tensor_tensor(out=xt[:, u, cols], in0=mbank[o][:, :], scalar=top[:, 3:4],
                                                 in1=xt[:, u, cols], op0=ALU.mult, op1=ALU.add).then_inc(result, 1)

                for n, kt in enumerate(LEFT):
                    for o in range(OC):
                        merge_add(dve, kt, o, stages[:, n, :], bank[4 * n + o])
                    if n == 1:
                        dve.wait_ge(w_scaled, kt)
                    merge_scale(dve, kt, stages[:, n, :])
                    if n == 0:
                        normalise(0, 0, 0)
                dve.wait_ge(wrow_step, W_STEPS * KT)
                dve.tensor_reduce(top[:, 0:1], wmax[:], AX_X, ALU.max).then_inc(top_max, 1)
                dve.wait_ge(top_all, 1)
                dve.reciprocal(top[:, 2:3], top[:, 1:2]).then_inc(top_step, 1)
                dve.tensor_scalar(top[:, 3:4], top[:, 1:2], 1.0 / (TOP * XS), None, ALU.mult).then_inc(top_step, 1)
                dve.wait_ge(top_step, 2)
                dve.tensor_scalar(fold[:], wmax[:], top[:, 2:3], None, ALU.mult).then_inc(fold_ok, 1)
                dve.wait_ge(fold_ok, 1)
                transposed_lo(0, 0)

                def body(r, i, u, ahead):
                    if ahead:
                        normalise(r + 1, i + u, 1 - u)
                    dve.wait_ge(biased, r + 1)
                    add_product(r, u, 0)
                    if ahead:
                        transposed_lo(r + 1, 1 - u)
                    add_product(r, u, 1)

                rows(dve, body)

            @block.scalar
            def _(act):
                def transposed_hi(r, u):
                    for k in range(KT):
                        if k % 4 == 0:
                            act.wait_ge(t_done, 4 * r + k // 4 + 1)
                        act.activation(yT[:, u, 0, k, :], tbank[k // 4][:, (k % 4) * P:(k % 4 + 1) * P], ACT.Copy,
                                       scale=fold[:, k:k + 1]).then_inc(y_hi, 1)

                act.wait_ge(x1_out, 16 * STEPS * B)
                merge_hi(act, LEFT[0], stages[:, 0, :])
                act.wait_ge(fold_ok, 1)
                transposed_hi(0, 0)
                merge_hi(act, LEFT[1], stages[:, 1, :])

                def body(r, i, u, ahead):
                    if ahead:
                        transposed_hi(r + 1, 1 - u)

                rows(act, body)

            @block.tensor
            def _(pe):
                def transposes(r):
                    pe.wait_ge(yn_done, r + 1)
                    for k in range(KT):
                        mm = pe.transpose(tbank[k // 4][:, (k % 4) * P:(k % 4 + 1) * P], yn[:, k * P:(k + 1) * P], ident[:])
                        if k % 4 == 3:
                            mm.then_inc(t_done, 1)

                def products(r, u, pair):
                    cols = [slice(o * NC, (o + 1) * NC) for o in (2 * pair, 2 * pair + 1)]
                    dst = [mbank[2 * pair + q][:, :] for q in range(2)]
                    for k in range(KT):
                        if pair == 0 and k in LEFT:
                            pe.wait_ge(w_lo, k + 1)
                        hi, lo = yT[:, u, 0, k, :], yT[:, u, 1, k, :]
                        for q in range(2):
                            pe.matmul(dst[q], hi, W[:, k, 0, cols[q]], start=(k == 0), stop=False)
                        for q in range(2):
                            pe.matmul(dst[q], hi, W[:, k, 1, cols[q]], start=False, stop=False)
                        for q in range(2):
                            mm = pe.matmul(dst[q], lo, W[:, k, 0, cols[q]], start=False, stop=(k == KT - 1))
                            if k == KT - 1:
                                mm.then_inc(mm_done, 1)

                pe.wait_ge(x1b, CT * STEPS * B)
                pe.wait_ge(stage_in, 32 * KT)
                for n in range(2):
                    for o in range(OC):
                        merge_product(pe, o, lora_as[:, n, :], bank[4 * n + o])
                pe.wait_ge(lora_added, OC * KT)
                transposes(0)

                def body(r, i, u, ahead):
                    pe.wait_ge(y_lo, KT * (r + 1))
                    products(r, u, 0)
                    if ahead:
                        transposes(r + 1)
                    else:
                        pe.wait_ge(result, OC * r)
                    products(r, u, 1)

                rows(pe, body)


def kernel(x, ctx_1024, L0_xattn_Wq, L0_xattn_Wk, L0_xattn_Wv, L0_xattn_Wskip, L0_ffn_lora_A, L0_ffn_lora_B,
           L0_ffn_W, L0_ffn_bias, L0_ffn_lora_weights):
    import numpy as np
    import concourse.bacc as bacc
    from concourse.bass_utils import run_bass_kernel_spmd

    c = np.ascontiguousarray
    n_lora, rank, d_in = L0_ffn_lora_A.shape
    d_out = L0_ffn_W.shape[0]
    ins = {
        "x": c(x), "ctx": c(ctx_1024), "wq": c(L0_xattn_Wq), "wk": c(L0_xattn_Wk),
        "wvT": c(np.transpose(L0_xattn_Wv)), "wskipT": c(np.transpose(L0_xattn_Wskip)),
        "lora_a": c(np.reshape(L0_ffn_lora_A, (n_lora * rank, d_in))),
        "lora_bT": c(np.reshape(np.transpose(L0_ffn_lora_B, (0, 2, 1)), (n_lora * rank, d_out))),
        "lora_w": c(np.reshape(np.repeat(L0_ffn_lora_weights, rank), (n_lora * rank, 1))),
        "wT": c(np.reshape(np.transpose(L0_ffn_W), (d_in // P, P, d_out))),
        "bias": c(L0_ffn_bias),
    }
    nc = bacc.Bacc("TRN2", target_bir_lowering=False, num_devices=1)
    aps = [nc.dram_tensor(f"in_{k}", a.shape, mybir.dt.from_np(a.dtype), kind="ExternalInput").ap()
           for k, a in ins.items()]
    x1 = nc.dram_tensor("x1", x.shape, F32, kind="Internal").ap()
    out = nc.dram_tensor("out_x", x.shape, F32, kind="ExternalOutput").ap()
    xattn_ffn(nc, *aps, x1, out)
    r = run_bass_kernel_spmd(nc, [{f"in_{k}": a for k, a in ins.items()}], core_ids=[0])
    return r.results[0]["out_x"]
```

```python
from collections import namedtuple
from contextlib import ExitStack

import concourse.bass as bass
from concourse import mybir


P = 128
NC = 512
EPS = 1e-5
LORA_SCALE = 2.0
XS = 2.0 ** 10
PS = 2.0 ** 14
TOP = 2.0 ** 14
TINY = 2.0 ** -100

ALU = mybir.AluOpType
ACT = mybir.ActivationFunctionType
AX_X = mybir.AxisListType.X
F16 = mybir.dt.float16
F32 = mybir.dt.float32
U32 = mybir.dt.uint32
ABSMAX = bass.bass_isa.ReduceOp.absmax
EXPONENT = 0x7F800000

Step = namedtuple("Step", "g b h p j")


def xattn_ffn(nc, x, ctx_, wq, wk, wvT, wskipT, lora_a, lora_bT, lora_w, wT, bias, x1, out):
    B, C, N = x.shape
    M = ctx_.shape[2]
    R = lora_a.shape[0]
    CT, MT, KT, OC = C // P, M // P, N // P, N // NC
    STEPS = N // NC
    NT = NC // P
    ROWS = B * C // P
    assert CT == 2 and M == NC and R == P and STEPS == 4 and B % 2 == 0 and ROWS % 2 == 0

    def step(b, h, p, j):
        return Step(STEPS * b + j, b, h, p, j)

    def after(s, n=1):
        for _ in range(n):
            if s.j < STEPS - 1:
                s = Step(s.g + 1, s.b, s.h, s.p, s.j + 1)
            else:
                s = Step(s.g + 1, s.b + 1, s.h + s.p, 1 - s.p, 0)
        return s

    LOOPED = KT - 5
    LATE = {(0, 0): KT - 5, (1, 0): KT - 4, (1, 1): KT - 3, (1, 2): KT - 2, (1, 3): KT - 1}
    LEFT = (KT - 2, KT - 1)

    def batches(eng, body):
        for lo, hi, merge in ((0, LOOPED // 2, 2), (LOOPED // 2, LOOPED // 2 + 1, 1), (LOOPED // 2 + 1, B // 2 - 1, 0)):
            with eng.Fori(lo, hi) as i:
                for p in range(2):
                    for j in range(STEPS):
                        body(step(2 * i + p, i, p, j), 2, 2 * i + p if p < merge else None, None, None)
        before = None
        for p in range(2):
            for j in range(STEPS):
                late = LATE.get((p, j))
                body(step(B - 2 + p, B // 2 - 1, p, j), 1 - p, None, late, before)
                before = late

    with ExitStack() as stack:
        def sb(name, shape, dt):
            return stack.enter_context(nc.sbuf_tensor(name, shape, dt))

        def sem(name):
            return stack.enter_context(nc.semaphore(name))

        bank = [stack.enter_context(nc.psum_tensor(f"bank{i}", [P, NC], F32)) for i in range(8)]

        W = sb("W", [P, KT, 2, N], F16)

        def spare(k0, k1):
            return W[:, k0:k1].rearrange("p k s n -> p (k s n)").bitcast(F32)

        xbuf = [spare(KT - 4 + 2 * p, KT - 2 + 2 * p).rearrange("p (t n) -> p t n", t=CT) for p in range(2)]
        raw = spare(KT - 5, KT - 4).rearrange("p (v n) -> p v n", v=2)
        ctx_raw = raw[:, 0, :]

        slots = sb("slots", [P, 8, N], F32)

        def slot(i, half=None):
            return slots[:, i, :] if half is None else slots[:, i, half * (N // 2):(half + 1) * (N // 2)]

        stages = [slot(0), slot(1)]
        mT_raw = slot(6, 0)[:, 0:CT * C].rearrange("p (t c) -> p t c", t=CT)
        wv_raw = slot(6, 0)[:, CT * C:2 * CT * C].rearrange("p (t c) -> p t c", t=CT)
        ctx_first = slot(6, 1).rearrange("p (t m) -> p t m", t=CT)
        qk_w = slot(0)[:, 0:2 * CT * C].rearrange("p (w t c) -> p w t c", w=2, t=CT)
        wsk_raw = slot(0)[:, 2 * CT * C:3 * CT * C]
        kk = [slot(i, 0).bitcast(F16).rearrange("p (q t m) -> p q t m", q=2, t=CT) for i in (1, 6)]
        vT = [slot(i, 1).bitcast(F16).rearrange("p (q t c) -> p q t c", q=2, t=MT) for i in (1, 6)]
        ctxs = slot(2, 0).bitcast(F16).rearrange("p (q t m) -> p q t m", q=2, t=CT)
        xn32 = slot(2, 1).rearrange("p (t n) -> p t n", t=CT)
        xt = [slot(2), slot(6)]
        prob = slot(3).rearrange("p (t m) -> p t m", t=NT)
        yn = slot(3)
        xn = slot(4).bitcast(F16).rearrange("p (b q t n) -> p b q t n", b=2, q=2, t=CT)
        pT = slot(5).bitcast(F16).rearrange("p (q m n) -> p q m n", q=2, m=MT)
        yT = [slot(i).bitcast(F16).rearrange("p (q k r) -> p q k r", q=2, k=KT) for i in (4, 5)]
        lora_b_sb = slot(7)
        bias_sb = slot(7)

        ident = sb("ident", [P, P], F32)
        lora_a_sb = sb("lora_a_sb", [P, 2, P], F32)
        coef = sb("coef", [P, 2], F32)
        carrier = sb("carrier", [P, 1], F32)
        wmax = sb("wmax", [P, KT], F32)
        wrow = sb("wrow", [P, 2, 4], F32)

        stage_in = [sem("stage_in0"), sem("stage_in1")]
        lora_done, lora_added = sem("lora_done"), sem("lora_added")
        wrow_step, w_scaled, w_hi, w_lo = sem("wrow_step"), sem("w_scaled"), sem("w_hi"), sem("w_lo")
        W_STEPS = 5
        SECOND = (KT - 3, KT - 1)

        def stage_of(kt):
            if isinstance(kt, int) and kt in SECOND:
                return 1, SECOND.index(kt) + 1
            return 0, kt if isinstance(kt, int) and kt > SECOND[0] else kt + 1

        def merge_load(sp, kt):
            u, _ = stage_of(kt)
            sp.dma_start(stages[u], wT[kt]).then_inc(stage_in[u], 16)
            sp.dma_start(lora_a_sb[:, u, :], lora_a[:, bass.ts(kt, P)]).then_inc(stage_in[u], 16)

        def merge_product(pe, kt, o, dst):
            pe.matmul(dst[:, :], lora_a_sb[:, stage_of(kt)[0], :], lora_b_sb[:, o * NC:(o + 1) * NC],
                      start=True, stop=True).then_inc(lora_done, 1)

        def merge_add(dve, kt, o, src):
            u, n = stage_of(kt)
            cols = slice(o * NC, (o + 1) * NC)
            dve.wait_ge(stage_in[u], 32 * n)
            dve.wait_ge(lora_done, OC * kt + o + 1)
            dve.tensor_tensor(stages[u][:, cols], src[:, :], stages[u][:, cols], ALU.add).then_inc(lora_added, 1)

        def merge_scale(dve, kt):
            u, _ = stage_of(kt)
            k = W_STEPS * kt
            dve.wait_ge(lora_added, OC * (kt + 1))
            dve.tensor_reduce(wrow[:, u, 0:1], stages[u], AX_X, ALU.max,
                              apply_absolute_value=True).then_inc(wrow_step, 1)
            dve.wait_ge(wrow_step, k + 1)
            dve.tensor_scalar(wrow[:, u, 1:2], wrow[:, u, 0:1], TINY, None, ALU.max).then_inc(wrow_step, 1)
            dve.wait_ge(wrow_step, k + 2)
            dve.tensor_scalar(wmax[:, bass.ds(kt, 1)].bitcast(U32), wrow[:, u, 1:2].bitcast(U32), EXPONENT,
                              None, ALU.bitwise_and).then_inc(wrow_step, 1)
            dve.wait_ge(wrow_step, k + 3)
            dve.tensor_scalar(wrow[:, u, 2:3], wmax[:, bass.ds(kt, 1)], 1.0 / TOP, None, ALU.mult).then_inc(wrow_step, 1)
            dve.wait_ge(wrow_step, k + 4)
            dve.reciprocal(wrow[:, u, 3:4], wrow[:, u, 2:3]).then_inc(wrow_step, 1)

        def half_of(kt, q):
            return W[:, bass.ds(kt, 1), q, :].rearrange("p k n -> p (k n)")

        def merge_scaled(act, kt):
            u, _ = stage_of(kt)
            act.wait_ge(wrow_step, W_STEPS * (kt + 1))
            act.activation(stages[u], stages[u], ACT.Copy, scale=wrow[:, u, 3:4]).then_inc(w_scaled, 1)

        def merge_hi(act, kt):
            u, _ = stage_of(kt)
            act.wait_ge(w_scaled, kt + 1)
            act.activation(half_of(kt, 0), stages[u], ACT.Copy).then_inc(w_hi, 1)

        def merge_lo(pool, kt):
            pool.wait_ge(w_hi, kt + 1)
            pool.tensor_tensor(half_of(kt, 1), stages[stage_of(kt)[0]], half_of(kt, 0),
                               ALU.subtract).then_inc(w_lo, 1)

        mT, wv_sb = sb("mT", [P, 2, CT, C], F16), sb("wv_sb", [P, 2, CT, C], F16)
        wsk = sb("wsk", [P, 2, CT, C], F16)
        skip32 = sb("skip32", [P, CT, NC], F32)
        stats = sb("stats", [P, CT, STEPS, 6], F32)
        mv = sb("mv", [P, 2, CT, 2], F32)
        veps = sb("veps", [P, CT], F32)
        half = sb("half", [P, CT], F32)
        rstd = sb("rstd", [P, 2, CT], F32)
        amax = sb("amax", [P, 2], F32)
        gmax = sb("gmax", [P, 2], F32)
        cmax = sb("cmax", [P, 2], F32)
        pow2 = sb("pow2", [P, 2], F32)
        unscale = sb("unscale", [P, 2], F32)
        kvscale = sb("kvscale", [P, 2], F32)
        escale = sb("escale", [P, 2], F32)
        vscale = sb("vscale", [P, 2], F32)
        wsk_sc = sb("wsk_sc", [P, 8], F32)
        wkv_sc = sb("wkv_sc", [P, 6, 2], F32)
        ctx_sc = sb("ctx_sc", [P, 6], F32)
        kv_un = sb("kv_un", [P, 2], F32)
        pool_carrier = sb("pool_carrier", [P, 1], F32)
        CTX_STEPS = 5
        rowmax = sb("rowmax", [P, NT], F32)
        nmax = sb("nmax", [P, NT], F32)
        rsum = sb("rsum", [P, NT], F32)
        rinv = sb("rinv", [P, NT], F32)
        KV_STEPS = 6
        KV_FIRST = 5
        ebank, sbank, abank = bank[0:4], bank[4:6], bank[6:8]

        w_in = sem("w_in")
        wv_in, wsk_in = sem("wv_in"), sem("wsk_in")
        lora_in = sem("lora_in")
        x_in = [[sem(f"x_in{p}{j}") for j in range(STEPS)] for p in range(2)]
        ctx_in = sem("ctx_in")
        x1_out = sem("x1_out")
        ident_zero, ident_ok = sem("ident_zero"), sem("ident_ok")
        half_ok, lora_b_ok = sem("half_ok"), sem("lora_b_ok")
        mT_done, mT_ok = sem("mT_done"), sem("mT_ok")
        wsk_max, wsk_all, wsk_step = sem("wsk_max"), sem("wsk_all"), sem("wsk_step")
        wsk_hi, wsk_lo = sem("wsk_hi"), sem("wsk_lo")
        coef_ok = sem("coef_ok")
        wkv_max, wkv_all, wkv_step = sem("wkv_max"), sem("wkv_all"), sem("wkv_step")
        wkv_hi, wkv_lo = sem("wkv_hi"), sem("wkv_lo")
        bn_done, mv_done, veps_done = sem("bn_done"), sem("mv_done"), sem("veps_done")
        rstd_done = sem("rstd_done")
        ctx_max, ctx_all, ctx_step = sem("ctx_max"), sem("ctx_all"), sem("ctx_step")
        ctx_scaled, ctx_hi, ctx_lo = sem("ctx_scaled"), sem("ctx_hi"), sem("ctx_lo")
        kk_done, v_done = sem("kk_done"), sem("v_done")
        kk_raw, v_raw = sem("kk_raw"), sem("v_raw")
        kv_max, kv_all, kv_step = sem("kv_max"), sem("kv_all"), sem("kv_step")
        kv_scaled, kv_hi, kv_lo = sem("kv_scaled"), sem("kv_hi"), sem("kv_lo")
        first_kv_hi = sem("first_kv_hi")
        xn_done, xn_hi, xn_lo = sem("xn_done"), sem("xn_hi"), sem("xn_lo")
        skip_done, skip_out, x1a = sem("skip_done"), sem("skip_out"), sem("x1a")
        att_done, x1b = sem("att_done"), sem("x1b")
        e_done, max_done, nmax_done = sem("e_done"), sem("max_done"), sem("nmax_done")
        exp_done, rinv_done, prob_done = sem("exp_done"), sem("rinv_done"), sem("prob_done")
        t_done, pT_hi, pT_lo = sem("t_done"), sem("pT_hi"), sem("pT_lo")

        x_v = x.rearrange("b (t p) n -> b p t n", p=P)
        x1_v = x1.rearrange("b (t p) n -> b p t n", p=P)
        ctx_v = ctx_.rearrange("b (t p) m -> b p t m", p=P)
        ctx_raw_v = ctx_raw.rearrange("p (t m) -> p t m", t=CT)

        def attention_sync(sp):
            def load_x(b):
                for j in range(STEPS):
                    cols = slice(j * NC, (j + 1) * NC)
                    sp.dma_start(xbuf[b][:, :, cols], x_v[b][:, :, cols]).then_inc(x_in[b][j], 16)

            sp.dma_start(qk_w[:, 0], wq.rearrange("(t p) c -> p t c", p=P)).then_inc(w_in, 16)
            load_x(0)
            sp.dma_start(lora_b_sb, lora_bT).then_inc(lora_in, 16)
            sp.dma_start(coef[:, 0:1], lora_w).then_inc(lora_in, 16)
            load_x(1)
            sp.wait_ge(kv_lo, 1)
            sp.dma_start(ctx_raw_v, ctx_v[1]).then_inc(ctx_in, 16)
            sp.wait_ge(mT_done, CT)
            sp.wait_ge(wsk_lo, 2)
            merge_load(sp, 0)

            def body(s, ahead, kt, late, before):
                cols = slice(s.j * NC, (s.j + 1) * NC)
                if ahead < 2 and s.j == 3 - s.p:
                    sp.wait_ge(w_lo, KT - 4 + 2 * s.p)
                    merge_load(sp, KT - 4 + 3 * s.p)
                sp.wait_ge(x1b, CT * (s.g + 1))
                sp.dma_start(x1_v[s.b][:, :, cols], xbuf[s.p][:, :, cols]).then_inc(x1_out, 16)
                if (s.p, s.j) == (0, 3) and ahead < 2:
                    merge_load(sp, KT - 3)
                sp.wait_ge(x1_out, 16 * (s.g + 1))
                if ahead == 2:
                    sp.dma_start(xbuf[s.p][:, :, cols], x_v[s.b + 2][:, :, cols]).then_inc(x_in[s.p][s.j], 16)
                    if s.j == 2:
                        sp.wait_ge(kv_lo, 2 * s.b + 3)
                        sp.dma_start(ctx_raw_v, ctx_v[s.b + 2]).then_inc(ctx_in, 16)
                    if kt is not None and s.j == 3:
                        sp.wait_ge(w_lo, kt + 1)
                        merge_load(sp, kt + 1)
                elif (s.p, s.j) == (1, 1):
                    sp.wait_ge(w_lo, KT - 3)
                    merge_load(sp, KT - 2)
                    sp.wait_ge(xn_lo, CT * STEPS * B)
                    sp.wait_ge(v_done, B)
                    sp.dma_start(xt[0], x1_r[0]).then_inc(xt_in[0], 16)

            batches(sp, body)

        def attention_scalar(act):
            act.dma_start(qk_w[:, 1], wk.rearrange("(t p) c -> p t c", p=P)).then_inc(w_in, 16)
            act.dma_start(ctx_first, ctx_v[0]).then_inc(ctx_in, 16)
            act.dma_start(wsk_raw.rearrange("p (t c) -> p t c", t=CT),
                          wskipT.rearrange("(t p) c -> p t c", p=P)).then_inc(wsk_in, 16)
            act.dma_start(wv_raw, wvT.rearrange("(t p) c -> p t c", p=P)).then_inc(wv_in, 16)
            act.wait_ge(mT_done, CT)
            for t in range(CT):
                last = act.activation(mT_raw[:, t, :], sbank[t][:, 0:C], ACT.Copy)
            last.then_inc(mT_ok, 1)

            def keys_raw(b, scale=1.0):
                act.wait_ge(kk_done, b + 1)
                for t in range(CT):
                    last = act.activation(raw[:, 0, t * M:(t + 1) * M], sbank[t][:, :], ACT.Copy, scale=scale)
                last.then_inc(kk_raw, 1)

            def values_raw(b, scale=1.0):
                act.wait_ge(v_done, b + 1)
                for t in range(2):
                    last = act.activation(raw[:, 1, t * NC:(t + 1) * NC], abank[t][:, :], ACT.Copy, scale=scale)
                last.then_inc(v_raw, 1)

            def context_hi(b):
                act.wait_ge(ctx_step, CTX_STEPS * b)
                act.activation(ctx_raw, ctx_raw, ACT.Copy, scale=ctx_sc[:, 5:6]).then_inc(ctx_scaled, 1)
                act.wait_ge(ctx_scaled, b)
                act.activation(ctxs[:, 0].rearrange("p t m -> p (t m)"), ctx_raw, ACT.Copy).then_inc(ctx_hi, 1)

            def first_hi(v):
                act.wait_ge(kv_step, KV_FIRST * (v + 1))
                hi = (kk, vT)[v][0][:, 0].rearrange("p t n -> p (t n)")
                for part in (slice(0, NC), slice(NC, 2 * NC)):
                    act.activation(hi[:, part], raw[:, v, part], ACT.Copy,
                                   scale=kvscale[:, v:v + 1]).then_inc(first_kv_hi, 1)

            def keys_values_hi(b, p, v):
                act.wait_ge(kv_step, 2 * KV_FIRST + KV_STEPS * b)
                act.activation(raw[:, v, :], raw[:, v, :], ACT.Copy, scale=kvscale[:, v:v + 1]).then_inc(kv_scaled, 1)
                act.wait_ge(kv_scaled, 2 * b + v - 1)
                act.activation((kk, vT)[v][p][:, 0].rearrange("p t n -> p (t n)"), raw[:, v, :],
                               ACT.Copy).then_inc(kv_hi, 1)

            def exponential(s, t):
                act.wait_ge(nmax_done, NT * s.g + t + 1)
                act.activation(prob[:, t, :], ebank[t][:, :], ACT.Exp, bias=nmax[:, t:t + 1],
                               scale=escale[:, s.p:s.p + 1], accum_out=rsum[:, t:t + 1]).then_inc(exp_done, 1)

            def exponentials(s):
                for t in range(NT):
                    exponential(s, t)

            def xn_hi_of(s):
                for t in range(CT):
                    act.wait_ge(xn_done, CT * s.g + t + 1)
                    act.activation(xn[:, s.j % 2, 0, t, :], xn32[:, t, :], ACT.Copy).then_inc(xn_hi, 1)

            first = step(0, 0, 0, 0)
            act.wait_ge(wsk_step, 4)
            act.activation(wsk[:, 0].rearrange("p t c -> p (t c)"), wsk_raw,
                           ACT.Copy, scale=wsk_sc[:, 5:6]).then_inc(wsk_hi, 1)
            keys_raw(0)
            xn_hi_of(first)
            first_hi(0)
            values_raw(0)
            xn_hi_of(after(first))
            act.wait_ge(lora_in, 32)
            act.wait_ge(coef_ok, 1)
            act.activation(lora_b_sb, lora_b_sb, ACT.Copy, scale=coef[:, 1:2]).then_inc(lora_b_ok, 1)
            for t in range(NT):
                exponential(first, t)
                if t in (1, 2):
                    act.wait_ge(wkv_step, 4)
                    act.activation((mT, wv_sb)[t - 1][:, 0], (mT_raw, wv_raw)[t - 1], ACT.Copy,
                                   scale=wkv_sc[:, 5, t - 1:t]).then_inc(wkv_hi, 1)
            first_hi(1)

            def body(s, ahead, kt, late, before):
                for t in range(NT):
                    act.wait_ge(t_done, NT * s.g + t + 1)
                    act.activation(pT[:, 0, :, t * P:(t + 1) * P],
                                   ebank[t][:, :].rearrange("p (m n) -> p m n", m=MT), ACT.Copy).then_inc(pT_hi, 1)
                if ahead == 1 and s.j == 3:
                    act.wait_ge(kv_lo, 2 * B)
                    merge_hi(act, KT - 5)
                act.wait_ge(pT_lo, NT * s.g + 1)
                for t in range(CT):
                    act.wait_ge(skip_done, CT * s.g + t + 1)
                    act.activation(skip32[:, t, :], sbank[t][:, :], ACT.Copy,
                                   scale=wsk_sc[:, 6:7]).then_inc(skip_out, 1)
                last = ahead == 0
                if last and s.j in (1, 2):
                    merge_scaled(act, before)
                if last and s.j == 1:
                    act.wait_ge(x1_out, 16 * STEPS * (B - 1))
                    merge_hi(act, before)
                if ahead and s.j == 0:
                    context_hi(s.b + 1)
                if ahead and s.j == 2:
                    keys_values_hi(s.b + 1, 1 - s.p, 0)
                if ahead == 2 and s.j == 3:
                    keys_values_hi(s.b + 1, 1 - s.p, 1)
                if not (last and s.j == 3):
                    exponentials(after(s))
                if not (last and s.j >= 2):
                    xn_hi_of(after(s, 2))
                if ahead and s.j == 0:
                    keys_raw(s.b + 1, kv_un[:, 0:1])
                    values_raw(s.b + 1, kv_un[:, 1:2])
                if ahead == 1 and s.j == 2:
                    keys_values_hi(s.b + 1, 1 - s.p, 1)
                if kt is not None and s.j == 3:
                    merge_scaled(act, kt)
                    merge_hi(act, kt)
                if before is not None and ahead:
                    merge_scaled(act, before)
                if last and s.j == 2:
                    merge_hi(act, before)

            batches(act, body)

        def attention_gpsimd(pool):
            pool.memset(ident[:], 0.0).then_inc(ident_zero, 1)
            pool.wait_ge(ident_zero, 1)
            pool.affine_select(out=ident[:], in_=ident[:], compare_op=ALU.not_equal, fill=1.0, base=0,
                               pattern=[[-1, P]], channel_multiplier=1).then_inc(ident_ok, 1)
            pool.memset(half[:], -0.5).then_inc(half_ok, 1)
            pool.wait_ge(half_ok, 1)

            def inverse_deviation(b, p):
                pool.wait_ge(veps_done, b + 1)
                pool.tensor_tensor(rstd[:, p, :], veps[:], half[:], ALU.pow).then_inc(rstd_done, 1)

            def carry_wait():
                pool.tensor_tensor(pool_carrier[:], half[:, 0:1], half[:, 1:2], ALU.subtract)

            def keys_values_max(cols=slice(0, 2)):
                pool.partition_all_reduce(gmax[:, cols], amax[:, cols], P, ABSMAX).then_inc(kv_all, 1)

            def keys_values_lo(b, p, v):
                pool.wait_ge(kv_hi, 2 * b + v - 1)
                hi, lo = ((kk, vT)[v][p][:, q].rearrange("p t n -> p (t n)") for q in range(2))
                pool.tensor_tensor(lo, raw[:, v, :], hi, ALU.subtract).then_inc(kv_lo, 1)

            def normalised_lo(s):
                for t in range(CT):
                    pool.wait_ge(xn_hi, CT * s.g + t + 1)
                    pool.tensor_tensor(xn[:, s.j % 2, 1, t, :], xn32[:, t, :], xn[:, s.j % 2, 0, t, :],
                                       ALU.subtract).then_inc(xn_lo, 1)

            first = step(0, 0, 0, 0)
            pool.wait_ge(wsk_max, 1)
            pool.partition_all_reduce(wsk_sc[:, 1:2], wsk_sc[:, 0:1], P, ABSMAX).then_inc(wsk_all, 1)
            inverse_deviation(0, 0)
            pool.wait_ge(kv_max, 1)
            keys_values_max(slice(0, 1))
            normalised_lo(first)
            pool.wait_ge(kv_max, 2)
            keys_values_max(slice(1, 2))
            normalised_lo(after(first))
            pool.wait_ge(wkv_max, 2)
            pool.partition_all_reduce(wkv_sc[:, 1, :], wkv_sc[:, 0, :], P, ABSMAX).then_inc(wkv_all, 1)

            def body(s, ahead, kt, late, before):
                last = ahead == 0
                cols = slice(s.j * NC, (s.j + 1) * NC)
                if ahead and s.j == 0:
                    pool.wait_ge(ctx_max, s.b + 1)
                    carry_wait()
                    pool.partition_all_reduce(ctx_sc[:, 1:2], ctx_sc[:, 0:1], P, ABSMAX).then_inc(ctx_all, 1)
                for t in range(CT):
                    pool.wait_ge(skip_out, CT * s.g + t + 1)
                    pool.tensor_tensor(xbuf[s.p][:, t, cols], xbuf[s.p][:, t, cols], skip32[:, t, :],
                                       ALU.add).then_inc(x1a, 1)
                if ahead and s.j == 1:
                    pool.wait_ge(kv_max, 2 * (s.b + 2))
                    carry_wait()
                    keys_values_max()
                if ahead and s.j == 0:
                    pool.wait_ge(ctx_hi, s.b + 1)
                    pool.tensor_tensor(ctxs[:, 1].rearrange("p t m -> p (t m)"), ctx_raw,
                                       ctxs[:, 0].rearrange("p t m -> p (t m)"), ALU.subtract).then_inc(ctx_lo, 1)
                if not (last and s.j >= 2):
                    normalised_lo(after(s, 2))
                if ahead and s.j == 1:
                    inverse_deviation(s.b + 1, 1 - s.p)
                if ahead and s.j == 2 or ahead == 2 and s.j == 3:
                    keys_values_lo(s.b + 1, 1 - s.p, s.j - 2)
                if ahead == 1 and s.j == 2:
                    keys_values_lo(s.b + 1, 1 - s.p, 1)
                if kt is not None and s.j == 3:
                    merge_lo(pool, kt)
                if last and before is not None and before is not LEFT[0]:
                    merge_lo(pool, before)
                if ahead == 1 and s.j == 3:
                    merge_lo(pool, KT - 5)
                if last and s.j == 2:
                    inverse_deviation_b(pool, 0)

            batches(pool, body)

        def attention_vector(dve):
            def chunk_stats(b, h, p, j):
                dve.wait_ge(x_in[p][j], 16 * (h + 1))
                for t in range(CT):
                    dve.bn_stats(stats[:, t, j, :], xbuf[p][:, t, j * NC:(j + 1) * NC]).then_inc(bn_done, 1)

            def batch_stats(b, p):
                dve.wait_ge(bn_done, CT * STEPS * (b + 1))
                dve.memset(carrier[:], 0.0)
                for t in range(CT):
                    dve.bn_aggr(mv[:, p, t, :], stats[:, t].rearrange("p j s -> p (j s)")).then_inc(mv_done, 1)
                dve.wait_ge(mv_done, CT * (b + 1))
                dve.tensor_scalar(veps[:], mv[:, p, :, 1], EPS, XS ** -2, ALU.add, ALU.mult).then_inc(veps_done, 1)

            def normalise(s):
                dve.wait_ge(rstd_done, s.b + 1)
                dve.wait_ge(xn_lo, CT * s.g)
                for t in range(CT):
                    dve.tensor_scalar(xn32[:, t, :], xbuf[s.p][:, t, s.j * NC:(s.j + 1) * NC],
                                      mv[:, s.p, t, 0:1], rstd[:, s.p, t:t + 1],
                                      ALU.subtract, ALU.mult).then_inc(xn_done, 1)

            def keys_values_amax(b, v):
                dve.wait_ge((kk_raw, v_raw)[v], b + 1)
                dve.tensor_reduce(amax[:, v:v + 1], raw[:, v, :], AX_X, ALU.max,
                                  apply_absolute_value=True).then_inc(kv_max, 1)

            def scales(v0, v1, p, k):
                dve.tensor_scalar(cmax[:, v0:v1], gmax[:, v0:v1], TINY, None, ALU.max).then_inc(kv_step, 1)
                dve.wait_ge(kv_step, k + 1)
                dve.tensor_scalar(pow2[:, v0:v1].bitcast(U32), cmax[:, v0:v1].bitcast(U32), EXPONENT, None,
                                  ALU.bitwise_and).then_inc(kv_step, 1)
                dve.wait_ge(kv_step, k + 2)
                dve.tensor_scalar(unscale[:, v0:v1], pow2[:, v0:v1], 1.0 / TOP, None, ALU.mult).then_inc(kv_step, 1)
                dve.wait_ge(kv_step, k + 3)
                dve.reciprocal(kvscale[:, v0:v1], unscale[:, v0:v1]).then_inc(kv_step, 1)
                if v0 == 0:
                    dve.tensor_scalar(escale[:, p:p + 1], unscale[:, 0:1], 1.0 / (XS * C ** 0.5), None,
                                      ALU.mult).then_inc(kv_step, 1)
                if v1 == 2:
                    dve.tensor_scalar(vscale[:, p:p + 1], unscale[:, 1:2], 1.0 / PS, None,
                                      ALU.mult).then_inc(kv_step, 1)

            def keys_values_scales(b, p):
                dve.wait_ge(kv_all, b + 2)
                scales(0, 2, p, 2 * KV_FIRST + KV_STEPS * (b - 1))
                dve.wait_ge(kv_step, 2 * KV_FIRST + KV_STEPS * b)

            def context_scales(b):
                k = CTX_STEPS * (b - 1)
                dve.wait_ge(ctx_all, b)
                dve.tensor_scalar(ctx_sc[:, 2:3], ctx_sc[:, 1:2], TINY, None, ALU.max).then_inc(ctx_step, 1)
                dve.wait_ge(ctx_step, k + 1)
                dve.tensor_scalar(ctx_sc[:, 3:4].bitcast(U32), ctx_sc[:, 2:3].bitcast(U32), EXPONENT, None,
                                  ALU.bitwise_and).then_inc(ctx_step, 1)
                dve.wait_ge(ctx_step, k + 2)
                dve.tensor_scalar(ctx_sc[:, 4:5], ctx_sc[:, 3:4], 1.0 / TOP, None, ALU.mult).then_inc(ctx_step, 1)
                dve.wait_ge(ctx_step, k + 3)
                dve.reciprocal(ctx_sc[:, 5:6], ctx_sc[:, 4:5]).then_inc(ctx_step, 1)
                dve.tensor_scalar(kv_un[:], wkv_sc[:, 4, :], ctx_sc[:, 4:5], None, ALU.mult).then_inc(ctx_step, 1)

            def first_scales(v):
                dve.wait_ge(kv_all, v + 1)
                scales(v, v + 1, 0, KV_FIRST * v)
                dve.wait_ge(kv_step, KV_FIRST * (v + 1))

            def first_lo(v):
                hi, lo = ((kk, vT)[v][0][:, q].rearrange("p t n -> p (t n)") for q in range(2))
                for n, part in enumerate((slice(0, NC), slice(NC, 2 * NC))):
                    dve.wait_ge(first_kv_hi, 2 * v + n + 1)
                    last = dve.scalar_tensor_tensor(out=lo[:, part], in0=raw[:, v, part], scalar=kvscale[:, v:v + 1],
                                                    in1=hi[:, part], op0=ALU.mult, op1=ALU.subtract)
                last.then_inc(kv_lo, 1)

            def negated_max(s, t):
                dve.wait_ge(e_done, NT * s.g + t + 1)
                dve.tensor_reduce(rowmax[:, t:t + 1], ebank[t][:, :], AX_X, ALU.max).then_inc(max_done, 1)
                dve.wait_ge(max_done, NT * s.g + t + 1)
                dve.tensor_scalar(nmax[:, t:t + 1], rowmax[:, t:t + 1], escale[:, s.p:s.p + 1], -1.0,
                                  ALU.mult, ALU.mult).then_inc(nmax_done, 1)

            def probabilities(s, t):
                dve.wait_ge(exp_done, NT * s.g + t + 1)
                dve.reciprocal(rinv[:, t:t + 1], rsum[:, t:t + 1]).then_inc(rinv_done, 1)
                dve.wait_ge(rinv_done, NT * s.g + t + 1)
                dve.tensor_scalar(prob[:, t, :], prob[:, t, :], rinv[:, t:t + 1], PS,
                                  ALU.mult, ALU.mult).then_inc(prob_done, 1)

            def softmax(s):
                negated_max(s, 0)
                negated_max(s, 1)
                for t in range(NT):
                    if t + 2 < NT:
                        negated_max(s, t + 2)
                    probabilities(s, t)

            first = step(0, 0, 0, 0)
            dve.wait_ge(wsk_in, 16)
            dve.tensor_reduce(wsk_sc[:, 0:1], wsk_raw, AX_X, ALU.max, apply_absolute_value=True).then_inc(wsk_max, 1)
            chunk_stats(0, 0, 0, 0)
            dve.wait_ge(wsk_all, 1)
            dve.tensor_scalar(wsk_sc[:, 2:3], wsk_sc[:, 1:2], TINY, None, ALU.max).then_inc(wsk_step, 1)
            dve.wait_ge(wsk_step, 1)
            dve.tensor_scalar(wsk_sc[:, 3:4].bitcast(U32), wsk_sc[:, 2:3].bitcast(U32), EXPONENT, None,
                              ALU.bitwise_and).then_inc(wsk_step, 1)
            dve.wait_ge(wsk_step, 2)
            dve.tensor_scalar(wsk_sc[:, 4:5], wsk_sc[:, 3:4], 1.0 / TOP, None, ALU.mult).then_inc(wsk_step, 1)
            dve.wait_ge(wsk_step, 3)
            dve.tensor_scalar(wsk_sc[:, 6:7], wsk_sc[:, 4:5], 1.0 / XS, None, ALU.mult).then_inc(wsk_lo, 1)
            dve.reciprocal(wsk_sc[:, 5:6], wsk_sc[:, 4:5]).then_inc(wsk_step, 1)
            chunk_stats(0, 0, 0, 1)
            dve.wait_ge(wsk_hi, 1)
            dve.scalar_tensor_tensor(out=wsk[:, 1].rearrange("p t c -> p (t c)"), in0=wsk_raw, scalar=wsk_sc[:, 5:6],
                                     in1=wsk[:, 0].rearrange("p t c -> p (t c)"),
                                     op0=ALU.mult, op1=ALU.subtract).then_inc(wsk_lo, 1)
            for j in range(2, STEPS):
                chunk_stats(0, 0, 0, j)
            batch_stats(0, 0)
            keys_values_amax(0, 0)
            normalise(first)
            first_scales(0)
            first_lo(0)
            normalise(after(first))
            dve.wait_ge(lora_in, 32)
            dve.tensor_scalar(coef[:, 1:2], coef[:, 0:1], LORA_SCALE, None, ALU.mult).then_inc(coef_ok, 1)
            keys_values_amax(0, 1)
            first_scales(1)
            negated_max(first, 0)
            for v, (ready, src) in enumerate(((mT_ok, mT_raw), (wv_in, wv_raw))):
                dve.wait_ge(ready, (1, 16)[v])
                dve.tensor_reduce(wkv_sc[:, 0, v:v + 1], src.rearrange("p t c -> p (t c)"), AX_X, ALU.max,
                                  apply_absolute_value=True).then_inc(wkv_max, 1)
            negated_max(first, 1)
            dve.wait_ge(wkv_all, 1)
            dve.tensor_scalar(wkv_sc[:, 2, :], wkv_sc[:, 1, :], TINY, None, ALU.max).then_inc(wkv_step, 1)
            dve.wait_ge(wkv_step, 1)
            dve.tensor_scalar(wkv_sc[:, 3, :].bitcast(U32), wkv_sc[:, 2, :].bitcast(U32), EXPONENT, None,
                              ALU.bitwise_and).then_inc(wkv_step, 1)
            dve.wait_ge(wkv_step, 2)
            dve.tensor_scalar(wkv_sc[:, 4, :], wkv_sc[:, 3, :], 1.0 / TOP, None, ALU.mult).then_inc(wkv_step, 1)
            dve.wait_ge(wkv_step, 3)
            dve.reciprocal(wkv_sc[:, 5, :], wkv_sc[:, 4, :]).then_inc(wkv_step, 1)
            for t in range(NT):
                if t + 2 < NT:
                    negated_max(first, t + 2)
                probabilities(first, t)
            first_lo(1)
            dve.wait_ge(wkv_step, 4)
            for v in range(2):
                dve.wait_ge(wkv_hi, v + 1)
                dst = (mT, wv_sb)[v]
                dve.scalar_tensor_tensor(out=dst[:, 1], in0=(mT_raw, wv_raw)[v], scalar=wkv_sc[:, 5, v:v + 1],
                                         in1=dst[:, 0], op0=ALU.mult, op1=ALU.subtract).then_inc(wkv_lo, 1)

            def body(s, ahead, kt, late, before):
                last = ahead == 0
                cols = slice(s.j * NC, (s.j + 1) * NC)
                for t in range(NT):
                    dve.wait_ge(pT_hi, NT * s.g + t + 1)
                    dve.tensor_tensor(pT[:, 1, :, t * P:(t + 1) * P],
                                      ebank[t][:, :].rearrange("p (m n) -> p m n", m=MT),
                                      pT[:, 0, :, t * P:(t + 1) * P], ALU.subtract).then_inc(pT_lo, 1)
                if ahead and s.j == 0:
                    dve.wait_ge(ctx_in, 16 * (s.b + 2))
                    dve.tensor_reduce(ctx_sc[:, 0:1], ctx_raw, AX_X, ALU.max,
                                      apply_absolute_value=True).then_inc(ctx_max, 1)
                if not (last and s.j >= 2):
                    dve.wait_ge(skip_done, CT * (s.g + 1))
                    normalise(after(s, 2))
                if ahead and s.j == 0:
                    context_scales(s.b + 1)
                    for j in range(2):
                        chunk_stats(s.b + 1, s.h + s.p, 1 - s.p, j)
                if ahead and s.j == 1:
                    for v in range(2):
                        keys_values_amax(s.b + 1, v)
                if kt is not None and s.j == 2:
                    merge_scale(dve, kt)
                if before is not None and before is not LEFT[0]:
                    merge_scale(dve, before)
                if not (last and s.j == 3):
                    softmax(after(s))
                if ahead and s.j == 1:
                    batch_stats(s.b + 1, 1 - s.p)
                if last and s.j == 2:
                    tile_stats(dve, 0, 0, 0)
                if last and s.j == 3:
                    dve.wait_ge(t_done, NT * STEPS * B)
                    tile_normalise(dve, 0, 0)
                    for o in range(OC):
                        merge_add(dve, late, o, bank[o])
                    merge_scale(dve, late)
                    weight_top(dve)
                for t in range(CT):
                    if last and s.j == 3 and t == 1:
                        weight_fold(dve)
                    dve.wait_ge(att_done, CT * s.g + t + 1)
                    dve.wait_ge(x1a, CT * s.g + t + 1)
                    dve.scalar_tensor_tensor(out=xbuf[s.p][:, t, cols], in0=abank[t][:, :],
                                             scalar=vscale[:, s.p:s.p + 1], in1=xbuf[s.p][:, t, cols],
                                             op0=ALU.mult, op1=ALU.add).then_inc(x1b, 1)
                if ahead and s.j == 0:
                    for j in range(2, STEPS):
                        chunk_stats(s.b + 1, s.h + s.p, 1 - s.p, j)
                if ahead and s.j == 1:
                    keys_values_scales(s.b + 1, 1 - s.p)
                merge = kt if s.j == 0 else None
                if late is not None and not (last and s.j == 3):
                    merge = late
                if merge is not None:
                    for o in range(OC):
                        merge_add(dve, merge, o, bank[4 + o])
                if last and s.j == 2:
                    merge_scale(dve, late)

            batches(dve, body)

        def attention_tensor(pe):
            def three_passes(dst, lhs, rhs, k, n):
                pe.matmul(dst, lhs[0], rhs[0], start=(k == 0), stop=False)
                pe.matmul(dst, lhs[0], rhs[1], start=False, stop=False)
                return pe.matmul(dst, lhs[1], rhs[0], start=False, stop=(k == n - 1))

            def keys(b):
                pe.wait_ge(ctx_lo, b)
                pe.wait_ge(wkv_lo, 2)
                for t in range(CT):
                    for k in range(CT):
                        mm = three_passes(sbank[t][:, :], [mT[:, q, k, t * P:(t + 1) * P] for q in range(2)],
                                          [ctxs[:, q, k, :] for q in range(2)], k, CT)
                mm.then_inc(kk_done, 1)

            def values(b, g):
                for m in range(MT):
                    if m % 2 == 0:
                        pe.wait_ge(x1b, CT * g + m // 2 + 1)
                    for k in range(CT):
                        mm = three_passes(abank[m // 2][:, (m % 2) * C:(m % 2 + 1) * C],
                                          [ctxs[:, q, k, m * P:(m + 1) * P] for q in range(2)],
                                          [wv_sb[:, q, k, :] for q in range(2)], k, CT)
                mm.then_inc(v_done, 1)

            def first_keys_values():
                pe.wait_ge(ctx_in, 16)
                for t in range(CT):
                    for k in range(CT):
                        mm = pe.matmul(sbank[t][:, :], mT_raw[:, k, t * P:(t + 1) * P], ctx_first[:, k, :],
                                       start=(k == 0), stop=(k == CT - 1))
                mm.then_inc(kk_done, 1)
                pe.wait_ge(wv_in, 16)
                for m in range(MT):
                    for k in range(CT):
                        mm = pe.matmul(abank[m // 2][:, (m % 2) * C:(m % 2 + 1) * C],
                                       ctx_first[:, k, m * P:(m + 1) * P], wv_raw[:, k, :],
                                       start=(k == 0), stop=(k == CT - 1))
                mm.then_inc(v_done, 1)

            def energies(s, first=False):
                pe.wait_ge(xn_lo, CT * (s.g + 1))
                pe.wait_ge(kv_lo, 2 * s.b + 1)
                for t in range(NT):
                    if not first:
                        pe.wait_ge(pT_lo, NT * (s.g - 1) + t + 1)
                    for k in range(CT):
                        mm = three_passes(ebank[t][:, :],
                                          [xn[:, s.j % 2, q, k, t * P:(t + 1) * P] for q in range(2)],
                                          [kk[s.p][:, q, k, :] for q in range(2)], k, CT)
                    mm.then_inc(e_done, 1)

            pe.wait_ge(w_in, 32)
            for t in range(CT):
                for k in range(CT):
                    mm = pe.matmul(sbank[t][:, 0:C], qk_w[:, 1, k, t * P:(t + 1) * P], qk_w[:, 0, k, :],
                                   start=(k == 0), stop=(k == CT - 1))
                mm.then_inc(mT_done, 1)
            pe.wait_ge(mT_ok, 1)
            first_keys_values()
            first = step(0, 0, 0, 0)
            energies(first, True)
            pe.wait_ge(ident_ok, 1)
            pe.wait_ge(wsk_lo, 2)

            def body(s, ahead, kt, late, before):
                for t in range(NT):
                    pe.wait_ge(prob_done, NT * s.g + t + 1)
                    for m in range(MT):
                        mm = pe.transpose(ebank[t][:, m * P:(m + 1) * P], prob[:, t, m * P:(m + 1) * P], ident[:])
                    mm.then_inc(t_done, 1)
                if s.j == 1:
                    pe.wait_ge(kk_raw, s.b + 1 + (ahead > 0))
                if kt is not None and s.j == 1:
                    pe.wait_ge(lora_added, OC * kt + 2)
                if before is not None:
                    pe.wait_ge(lora_added, OC * before + 2)
                for t in range(CT):
                    for k in range(CT):
                        mm = three_passes(sbank[t][:, :],
                                          [wsk[:, q, k, t * P:(t + 1) * P] for q in range(2)],
                                          [xn[:, s.j % 2, q, k, :] for q in range(2)], k, CT)
                    mm.then_inc(skip_done, 1)
                if ahead or s.j < 3:
                    energies(after(s))
                if ahead == 0 and s.j == 3:
                    pe.wait_ge(stage_in[stage_of(late)[0]], 32 * stage_of(late)[1])
                    for o in range(OC):
                        pe.wait_ge(pT_lo, NT * s.g + o + 1)
                        merge_product(pe, late, o, bank[o])
                pe.wait_ge(pT_lo, NT * (s.g + 1))
                pe.wait_ge(kv_lo, 2 * s.b + 2)
                if s.j == 1:
                    pe.wait_ge(v_raw, s.b + 1 + (ahead > 0))
                for t in range(CT):
                    if ahead == 0 and s.j == 3 and t == 1:
                        pe.wait_ge(lora_added, OC * KT)
                        transposes(pe, 0)
                    for m in range(MT):
                        mm = three_passes(abank[t][:, :],
                                          [vT[s.p][:, q, m, t * P:(t + 1) * P] for q in range(2)],
                                          [pT[:, q, m, :] for q in range(2)], m, MT)
                    mm.then_inc(att_done, 1)
                if ahead and s.j == 0:
                    pe.wait_ge(skip_out, CT * (s.g + 1))
                    keys(s.b + 1)
                    values(s.b + 1, s.g)
                merge = kt if s.j == 0 else None
                if late is not None and not (ahead == 0 and s.j == 3):
                    merge = late
                if merge is not None:
                    pe.wait_ge(lora_b_ok, 1)
                    pe.wait_ge(stage_in[stage_of(merge)[0]], 32 * stage_of(merge)[1])
                    pe.wait_ge(skip_out, CT * (s.g + 1))
                    if ahead and s.j == 0:
                        pe.wait_ge(kk_raw, s.b + 2)
                    for o in range(OC):
                        if o >= 2:
                            pe.wait_ge(x1b, CT * s.g + o - 1)
                        if o == 2 and ahead and s.j == 0:
                            pe.wait_ge(v_raw, s.b + 2)
                        merge_product(pe, merge, o, bank[4 + o])

            batches(pe, body)

        b_stats = sb("stats2", [P, OC, 6], F32)
        b_mv = sb("mv2", [P, 2], F32)
        b_veps = sb("veps2", [P, 1], F32)
        b_rstd = sb("rstd2", [P, 1], F32)
        fold = sb("fold", [P, KT], F32)
        top = sb("top", [P, 4], F32)
        tbank, mbank = bank[0:4], bank[4:8]

        xt_in = [sem(f"xt_in{u}") for u in range(2)]
        bias_in = sem("bias_in")
        out_done = sem("out_done")
        top_max, top_all, top_step = (sem(n) for n in ("top_max", "top_all", "top_step"))
        fold_ok = sem("fold_ok")
        b_bn_done, b_mv_done, b_veps_done, b_rstd_done = (sem(n) for n in ("bn2", "mv2_done", "veps2_done", "rstd2_done"))
        yn_done, biased = sem("yn_done"), sem("biased")
        b_t_done, y_hi, y_lo = sem("t2_done"), sem("y_hi"), sem("y_lo")
        mm_done, result = sem("mm_done"), sem("result")
        x1_r = x1.rearrange("b (t p) n -> (b t) p n", p=P)
        out_r = out.rearrange("b (t p) n -> (b t) p n", p=P)
        HALF = N // 2

        def rows(eng, body):
            with eng.Fori(0, ROWS // 2 - 1) as i:
                for u in range(2):
                    body(2 * i + u, i, u, 2)
            for u in range(2):
                body(ROWS - 2 + u, ROWS // 2 - 1, u, 1 - u)

        def ffn_sync(sp):
            sp.wait_ge(att_done, CT * STEPS * B)
            sp.dma_start(xt[1], x1_r[1]).then_inc(xt_in[1], 16)
            sp.wait_ge(lora_done, OC * KT)
            sp.dma_start(bias_sb, bias.partition_broadcast(P)).then_inc(bias_in, 16)

            def body(r, i, u, ahead):
                for q in range(2):
                    sp.wait_ge(result, OC * r + 2 * (q + 1))
                    sp.dma_start(out_r[r][:, q * HALF:(q + 1) * HALF],
                                 xt[u][:, q * HALF:(q + 1) * HALF]).then_inc(out_done, 16)
                sp.wait_ge(out_done, 32 * (r + 1))
                if ahead == 2:
                    sp.dma_start(xt[u], x1_r[r + 2]).then_inc(xt_in[u], 16)

            rows(sp, body)

        def inverse_deviation_b(pool, r):
            pool.wait_ge(b_veps_done, r + 1)
            pool.tensor_tensor(b_rstd[:], b_veps[:], half[:, 0:1], ALU.pow).then_inc(b_rstd_done, 1)

        def ffn_gpsimd(pool):
            def add_bias(r, u):
                pool.wait_ge(yn_done, r + 1)
                pool.tensor_tensor(xt[u], xt[u], bias_sb, ALU.add).then_inc(biased, 1)

            pool.wait_ge(top_max, 1)
            pool.partition_all_reduce(top[:, 1:2], top[:, 0:1], P, ABSMAX).then_inc(top_all, 1)
            for kt in LEFT:
                merge_lo(pool, kt)
            pool.wait_ge(bias_in, 16)
            add_bias(0, 0)

            def body(r, i, u, ahead):
                if ahead:
                    inverse_deviation_b(pool, r + 1)
                    add_bias(r + 1, 1 - u)

            rows(pool, body)

        def tile_stats(dve, r, i, u):
            dve.wait_ge(xt_in[u], 16 * (i + 1))
            for o in range(OC):
                dve.bn_stats(b_stats[:, o, :], xt[u][:, o * NC:(o + 1) * NC]).then_inc(b_bn_done, 1)
            dve.wait_ge(b_bn_done, OC * (r + 1))
            dve.memset(carrier[:], 0.0)
            dve.bn_aggr(b_mv[:], b_stats[:].rearrange("p o s -> p (o s)")).then_inc(b_mv_done, 1)
            dve.wait_ge(b_mv_done, r + 1)
            dve.tensor_scalar(b_veps[:], b_mv[:, 1:2], EPS, XS ** -2, ALU.add, ALU.mult).then_inc(b_veps_done, 1)

        def tile_normalise(dve, r, u):
            dve.wait_ge(b_rstd_done, r + 1)
            dve.tensor_scalar(yn, xt[u], b_mv[:, 0:1], b_rstd[:, 0:1], ALU.subtract, ALU.mult).then_inc(yn_done, 1)

        def weight_top(dve):
            dve.wait_ge(wrow_step, W_STEPS * KT)
            dve.tensor_reduce(top[:, 0:1], wmax[:], AX_X, ALU.max).then_inc(top_max, 1)

        def weight_fold(dve):
            dve.wait_ge(top_all, 1)
            dve.reciprocal(top[:, 2:3], top[:, 1:2]).then_inc(top_step, 1)
            dve.tensor_scalar(top[:, 3:4], top[:, 1:2], 1.0 / (TOP * XS), None, ALU.mult).then_inc(top_step, 1)
            dve.wait_ge(top_step, 2)
            dve.tensor_scalar(fold[:], wmax[:], top[:, 2:3], None, ALU.mult).then_inc(fold_ok, 1)

        def ffn_vector(dve):
            def transposed_lo(r, u):
                for k in range(KT):
                    if k % 4 == 0:
                        dve.wait_ge(y_hi, KT * r + k + 4)
                    dve.scalar_tensor_tensor(out=yT[u][:, 1, k, :], in0=tbank[k // 4][:, (k % 4) * P:(k % 4 + 1) * P],
                                             scalar=fold[:, k:k + 1], in1=yT[u][:, 0, k, :],
                                             op0=ALU.mult, op1=ALU.subtract).then_inc(y_lo, 1)

            def add_product(r, u, pair):
                for o in (2 * pair, 2 * pair + 1):
                    cols = slice(o * NC, (o + 1) * NC)
                    dve.wait_ge(mm_done, OC * r + o + 1)
                    dve.scalar_tensor_tensor(out=xt[u][:, cols], in0=mbank[o][:, :], scalar=top[:, 3:4],
                                             in1=xt[u][:, cols], op0=ALU.mult, op1=ALU.add).then_inc(result, 1)

            dve.wait_ge(fold_ok, 1)
            transposed_lo(0, 0)

            def body(r, i, u, ahead):
                if ahead:
                    tile_stats(dve, r + 1, i + u, 1 - u)
                    dve.wait_ge(b_t_done, 4 * (r + 1))
                    tile_normalise(dve, r + 1, 1 - u)
                dve.wait_ge(biased, r + 1)
                add_product(r, u, 0)
                if ahead:
                    transposed_lo(r + 1, 1 - u)
                add_product(r, u, 1)

            rows(dve, body)

        def ffn_scalar(act):
            def transposed_hi(r, u):
                for k in range(KT):
                    if k % 4 == 0:
                        act.wait_ge(b_t_done, 4 * r + k // 4 + 1)
                    act.activation(yT[u][:, 0, k, :], tbank[k // 4][:, (k % 4) * P:(k % 4 + 1) * P], ACT.Copy,
                                   scale=fold[:, k:k + 1]).then_inc(y_hi, 1)

            act.wait_ge(fold_ok, 1)
            transposed_hi(0, 0)
            act.wait_ge(x1_out, 16 * STEPS * B)
            for kt in LEFT:
                merge_scaled(act, kt)
                merge_hi(act, kt)

            def body(r, i, u, ahead):
                if ahead:
                    transposed_hi(r + 1, 1 - u)

            rows(act, body)

        def transposes(pe, r):
            pe.wait_ge(yn_done, r + 1)
            for k in range(KT):
                mm = pe.transpose(tbank[k // 4][:, (k % 4) * P:(k % 4 + 1) * P], yn[:, k * P:(k + 1) * P], ident[:])
                if k % 4 == 3:
                    mm.then_inc(b_t_done, 1)

        def ffn_tensor(pe):
            def products(r, u, pair):
                cols = [slice(o * NC, (o + 1) * NC) for o in (2 * pair, 2 * pair + 1)]
                dst = [mbank[2 * pair + q][:, :] for q in range(2)]
                for k in range(KT):
                    if pair == 0 and k % 4 == 0:
                        pe.wait_ge(y_lo, KT * r + k + 4)
                    if pair == 0 and k in LEFT:
                        pe.wait_ge(w_lo, k + 1)
                    hi, lo = yT[u][:, 0, k, :], yT[u][:, 1, k, :]
                    for q in range(2):
                        pe.matmul(dst[q], hi, W[:, k, 0, cols[q]], start=(k == 0), stop=False)
                    for q in range(2):
                        pe.matmul(dst[q], hi, W[:, k, 1, cols[q]], start=False, stop=False)
                    for q in range(2):
                        mm = pe.matmul(dst[q], lo, W[:, k, 0, cols[q]], start=False, stop=(k == KT - 1))
                        if k == KT - 1:
                            mm.then_inc(mm_done, 1)

            def body(r, i, u, ahead):
                products(r, u, 0)
                if ahead:
                    transposes(pe, r + 1)
                else:
                    pe.wait_ge(result, OC * r)
                products(r, u, 1)

            rows(pe, body)

        block = stack.enter_context(nc.Block())

        @block.sync
        def _(sp):
            attention_sync(sp)
            ffn_sync(sp)

        @block.scalar
        def _(act):
            attention_scalar(act)
            ffn_scalar(act)

        @block.gpsimd
        def _(pool):
            attention_gpsimd(pool)
            ffn_gpsimd(pool)

        @block.vector
        def _(dve):
            attention_vector(dve)
            ffn_vector(dve)

        @block.tensor
        def _(pe):
            attention_tensor(pe)
            ffn_tensor(pe)


def kernel(x, ctx_1024, L0_xattn_Wq, L0_xattn_Wk, L0_xattn_Wv, L0_xattn_Wskip, L0_ffn_lora_A, L0_ffn_lora_B,
           L0_ffn_W, L0_ffn_bias, L0_ffn_lora_weights):
    import numpy as np
    import concourse.bacc as bacc
    from concourse.bass_utils import run_bass_kernel_spmd

    c = np.ascontiguousarray
    n_lora, rank, d_in = L0_ffn_lora_A.shape
    d_out = L0_ffn_W.shape[0]
    ins = {
        "x": c(x), "ctx": c(ctx_1024), "wq": c(L0_xattn_Wq), "wk": c(L0_xattn_Wk),
        "wvT": c(np.transpose(L0_xattn_Wv)), "wskipT": c(np.transpose(L0_xattn_Wskip)),
        "lora_a": c(np.reshape(L0_ffn_lora_A, (n_lora * rank, d_in))),
        "lora_bT": c(np.reshape(np.transpose(L0_ffn_lora_B, (0, 2, 1)), (n_lora * rank, d_out))),
        "lora_w": c(np.reshape(np.repeat(L0_ffn_lora_weights, rank), (n_lora * rank, 1))),
        "wT": c(np.reshape(np.transpose(L0_ffn_W), (d_in // P, P, d_out))),
        "bias": c(L0_ffn_bias),
    }
    nc = bacc.Bacc("TRN2", target_bir_lowering=False, num_devices=1)
    aps = [nc.dram_tensor(f"in_{k}", a.shape, mybir.dt.from_np(a.dtype), kind="ExternalInput").ap()
           for k, a in ins.items()]
    x1 = nc.dram_tensor("x1", x.shape, F32, kind="Internal").ap()
    out = nc.dram_tensor("out_x", x.shape, F32, kind="ExternalOutput").ap()
    xattn_ffn(nc, *aps, x1, out)
    r = run_bass_kernel_spmd(nc, [{f"in_{k}": a for k, a in ins.items()}], core_ids=[0])
    return r.results[0]["out_x"]
```
